# Optimizing a Trainium2 kernel written in Bass

```python
import numpy as np
import jax
import jax.numpy as jnp

def _softmax(x, axis=-1):
    return jax.nn.softmax(x, axis=axis)

def _gelu(x):
    return jax.nn.gelu(x, approximate=True)

def _silu(x):
    return jax.nn.silu(x)

def _sigmoid(x):
    return jax.nn.sigmoid(x)

def _layernorm(x, axis=-1, eps=1e-05):
    m = jnp.mean(x, axis=axis, keepdims=True)
    v = jnp.var(x, axis=axis, keepdims=True)
    return (x - m) / jnp.sqrt(v + eps)

def _scatter_add(tgt, idx, src, axis=0):
    return tgt.at[idx].add(src)

def _segment_sum(src, seg, n):
    return jax.ops.segment_sum(src, seg, n)
kernel_name = 'mk_perceiver_d1_seqx_r4_8da7d9'

def setup_inputs(seed: int=0):
    np.random.seed(seed)
    _w = jnp.asarray

    def _rec_inputs():
        import jax
        import jax.numpy as jnp
        _rk = jax.random.key(seed)
        x = -0.0002928 + 1 * jax.random.normal(jax.random.fold_in(_rk, 1), (2, 256, 512), jnp.float32)
        _lenS = 256 - jax.random.randint(jax.random.fold_in(_rk, 7), (2,), 0, max(1, 256 // 4) + 1, jnp.int32)
        _lenS2 = 4096 - jax.random.randint(jax.random.fold_in(_rk, 8), (2,), 0, max(1, 4096 // 4) + 1, jnp.int32)
        _ctx_512P = jax.random.normal(jax.random.fold_in(_rk, 11), (2, 16, 128), jnp.float32)
        _ctx_512c = jax.random.dirichlet(jax.random.fold_in(_rk, 511), 0.3 * jnp.ones((16,), jnp.float32), (2, 4096))
        _ctx_512t = jnp.einsum('bsk,bkd->bsd', _ctx_512c, _ctx_512P)
        _ctx_512t = _ctx_512t * jax.lax.rsqrt(jnp.mean(jnp.square(_ctx_512t)) + 1e-12) * 0.953939
        ctx_512 = 0.000227908 + 0.99994 * (_ctx_512t + 0.3 * jax.random.normal(jax.random.fold_in(_rk, 611), (2, 4096, 128), jnp.float32))
        return (x, ctx_512)
    x, ctx_512 = _rec_inputs()

    def _L0_xattn_setup():
        import jax, jax.numpy as jnp
        import numpy as np
        B, S, L = (2, 256, 256)
        DIM_Q, H, K, D_C, D_CQ, R = (512, 16, 128, 128, 384, 64)

        def _rope_tables(length, dim):
            inv = 1.0 / 10000.0 ** (jnp.arange(0, dim, 2, dtype=jnp.float32) / dim)
            f = jnp.arange(length, dtype=jnp.float32)[:, None] * inv[None, :]
            sin = jnp.repeat(jnp.sin(f), 2, axis=-1)
            cos = jnp.repeat(jnp.cos(f), 2, axis=-1)
            return (sin, cos)

        def _rotate_half(x):
            half = x.shape[-1] // 2
            return jnp.concatenate([-x[..., half:], x[..., :half]], axis=-1)

        def _apply_rope(x, sin, cos):
            return x * cos + _rotate_half(x) * sin
        key = jax.random.key(seed)
        ks = jax.random.split(key, 8)
        return {'hidden_q': jax.random.normal(ks[0], (B, S, DIM_Q), jnp.float32), 'kv_c': jax.random.normal(ks[1], (B, L, D_C), jnp.float32), 'Wq': jax.random.normal(ks[2], (H * K, DIM_Q), jnp.float32) / np.sqrt(DIM_Q).astype(np.float32), 'w_kc_q': jax.random.normal(ks[3], (H, K, D_CQ), jnp.float32) / np.sqrt(K).astype(np.float32), 'w_kc_kv': jax.random.normal(ks[4], (H, K, D_C), jnp.float32) / np.sqrt(K).astype(np.float32), 'W_qr': jax.random.normal(ks[5], (H, D_CQ, R), jnp.float32) / np.float32(np.sqrt(D_CQ) * np.sqrt(R)), 'W_kr': jax.random.normal(ks[6], (H, D_C, R), jnp.float32) / np.sqrt(D_C).astype(np.float32), 'Wo': jax.random.normal(ks[7], (DIM_Q, H * K), jnp.float32) / np.sqrt(H * K).astype(np.float32)}
    _L0_xattn_all = _L0_xattn_setup()
    _L0_xattn_in = {k: v for k, v in _L0_xattn_all.items() if k in ('Wq', 'w_kc_q', 'w_kc_kv', 'W_qr', 'W_kr', 'Wo')}
    del _L0_xattn_all

    def _L0_attn_setup():
        import jax, jax.numpy as jnp
        import numpy as np
        B, N, D = (4, 1024, 512)
        H = 16
        KH = 16
        DK = D // H
        key = jax.random.key(seed)
        kx, kq, kk, kv, ko = jax.random.split(key, 5)
        s = 1.0 / np.sqrt(D).astype(np.float32)
        return {'x': jax.random.normal(kx, (B, N, D), jnp.float32), 'Wq': jax.random.normal(kq, (D, D), jnp.float32) * s, 'Wk': jax.random.normal(kk, (D, D), jnp.float32) * s, 'Wv': jax.random.normal(kv, (D, D), jnp.float32) * s, 'Wo': jax.random.normal(ko, (D, D), jnp.float32) * s}
    _L0_attn_all = _L0_attn_setup()
    _L0_attn_in = {k: v for k, v in _L0_attn_all.items() if k in ('Wq', 'Wk', 'Wv', 'Wo')}
    del _L0_attn_all

    def _L0_ffn_setup():
        import jax, jax.numpy as jnp
        import numpy as np
        DIM = 512
        HID = 1408
        ZERO_POINT = 128.0

        def _qlinear(x, wq, scale):
            W = (wq.astype(jnp.float32) - ZERO_POINT) * scale[:, None]
            return jnp.einsum('bsd,hd->bsh', x, W)
        key = jax.random.key(seed)
        ks = jax.random.split(key, 7)
        B, S = (4, 512)
        sg = jax.random.uniform(ks[1], (HID,)) * (0.02 / np.sqrt(DIM)) + 0.0001
        su = jax.random.uniform(ks[3], (HID,)) * (0.02 / np.sqrt(DIM)) + 0.0001
        sd = jax.random.uniform(ks[5], (DIM,)) * (0.02 / np.sqrt(HID)) + 0.0001
        return {'x': jax.random.normal(ks[0], (B, S, DIM), dtype=jnp.float32), 'wq_gate': jax.random.randint(ks[2], (HID, DIM), 0, 64, dtype=jnp.int32), 's_gate': sg, 'wq_up': jax.random.randint(ks[4], (HID, DIM), 0, 64, dtype=jnp.int32), 's_up': su, 'wq_down': jax.random.randint(ks[6], (DIM, HID), 0, 64, dtype=jnp.int32), 's_down': sd}
    _L0_ffn_all = _L0_ffn_setup()
    _L0_ffn_in = {k: v for k, v in _L0_ffn_all.items() if k in ('wq_gate', 's_gate', 'wq_up', 's_up', 'wq_down', 's_down')}
    del _L0_ffn_all
    return {'x': x, 'ctx_512': ctx_512, 'L0_xattn_Wq': _L0_xattn_in['Wq'], 'L0_xattn_w_kc_q': _L0_xattn_in['w_kc_q'], 'L0_xattn_w_kc_kv': _L0_xattn_in['w_kc_kv'], 'L0_xattn_W_qr': _L0_xattn_in['W_qr'], 'L0_xattn_W_kr': _L0_xattn_in['W_kr'], 'L0_xattn_Wo': _L0_xattn_in['Wo'], 'L0_attn_Wq': _L0_attn_in['Wq'], 'L0_attn_Wk': _L0_attn_in['Wk'], 'L0_attn_Wv': _L0_attn_in['Wv'], 'L0_attn_Wo': _L0_attn_in['Wo'], 'L0_ffn_wq_gate': _L0_ffn_in['wq_gate'], 'L0_ffn_s_gate': _L0_ffn_in['s_gate'], 'L0_ffn_wq_up': _L0_ffn_in['wq_up'], 'L0_ffn_s_up': _L0_ffn_in['s_up'], 'L0_ffn_wq_down': _L0_ffn_in['wq_down'], 'L0_ffn_s_down': _L0_ffn_in['s_down']}

def reference(x, ctx_512, L0_xattn_Wq, L0_xattn_w_kc_q, L0_xattn_w_kc_kv, L0_xattn_W_qr, L0_xattn_W_kr, L0_xattn_Wo, L0_attn_Wq, L0_attn_Wk, L0_attn_Wv, L0_attn_Wo, L0_ffn_wq_gate, L0_ffn_s_gate, L0_ffn_wq_up, L0_ffn_s_up, L0_ffn_wq_down, L0_ffn_s_down):
    import jax
    import jax.numpy as jnp

    def _L0_xattn_ref(hidden_q, kv_c, Wq, w_kc_q, w_kc_kv, W_qr, W_kr, Wo):
        import jax, jax.numpy as jnp
        import numpy as np
        B, S, L = (2, 256, 256)
        DIM_Q, H, K, D_C, D_CQ, R = (512, 16, 128, 128, 384, 64)

        def _rope_tables(length, dim):
            inv = 1.0 / 10000.0 ** (jnp.arange(0, dim, 2, dtype=jnp.float32) / dim)
            f = jnp.arange(length, dtype=jnp.float32)[:, None] * inv[None, :]
            sin = jnp.repeat(jnp.sin(f), 2, axis=-1)
            cos = jnp.repeat(jnp.cos(f), 2, axis=-1)
            return (sin, cos)

        def _rotate_half(x):
            half = x.shape[-1] // 2
            return jnp.concatenate([-x[..., half:], x[..., :half]], axis=-1)

        def _apply_rope(x, sin, cos):
            return x * cos + _rotate_half(x) * sin
        Bv, Sv, _ = hidden_q.shape
        _, Lv, _ = kv_c.shape
        q_hk = (hidden_q @ Wq.T).reshape(Bv, Sv, H, K)
        q_big = jnp.einsum('bshk,hkq->bshq', q_hk, w_kc_q)
        sin_q, cos_q = _rope_tables(Sv, D_CQ)
        q_big = _apply_rope(q_big, sin_q[None, :, None, :], cos_q[None, :, None, :])
        sin_k, cos_k = _rope_tables(Lv, D_C)
        kv_r = _apply_rope(kv_c, sin_k[None], cos_k[None])
        q_r = jnp.einsum('bshq,hqr->bhsr', q_big, W_qr)
        k_r = jnp.einsum('bld,hdr->bhlr', kv_r, W_kr)
        scores = jnp.einsum('bhsr,bhlr->bhsl', q_r, k_r)
        attn = jax.nn.softmax(scores, axis=-1)
        ctx_c = jnp.einsum('bhsl,bld->bhsd', attn, kv_r)
        ctx_lat = jnp.einsum('bhsd,hkd->bhsk', ctx_c, w_kc_kv)
        ctx = ctx_lat.transpose(0, 2, 1, 3).reshape(Bv, Sv, H * K)
        return ctx @ Wo.T

    def _L0_attn_ref(x, Wq, Wk, Wv, Wo):
        import jax, jax.numpy as jnp
        import numpy as np
        B, N, D = (4, 1024, 512)
        H = 16
        KH = 16
        DK = D // H
        b, n, d = x.shape
        q = (x @ Wq).reshape(b, n, H, DK)
        k = (x @ Wk).reshape(b, n, KH, DK)
        v = (x @ Wv).reshape(b, n, KH, DK)
        scores = jnp.einsum('bnhd,bnkd->bnhk', q, k)
        o = jnp.einsum('bnhk,bnkd->bnhd', scores, v)
        return o.reshape(b, n, d) @ Wo

    def _L0_ffn_ref(x, wq_gate, s_gate, wq_up, s_up, wq_down, s_down):
        import jax, jax.numpy as jnp
        import numpy as np
        DIM = 512
        HID = 1408
        ZERO_POINT = 128.0

        def _qlinear(x, wq, scale):
            W = (wq.astype(jnp.float32) - ZERO_POINT) * scale[:, None]
            return jnp.einsum('bsd,hd->bsh', x, W)
        gate = _qlinear(x, wq_gate, s_gate)
        gate = jax.nn.silu(gate)
        up = _qlinear(x, wq_up, s_up)
        return _qlinear(gate * up, wq_down, s_down)
    x = x + _L0_xattn_ref(_layernorm(x, axis=-1), ctx_512, L0_xattn_Wq, L0_xattn_w_kc_q, L0_xattn_w_kc_kv, L0_xattn_W_qr, L0_xattn_W_kr, L0_xattn_Wo)
    x = x + _L0_attn_ref(_layernorm(x, axis=-1), L0_attn_Wq, L0_attn_Wk, L0_attn_Wv, L0_attn_Wo)
    x = x + _L0_ffn_ref(_layernorm(x, axis=-1), L0_ffn_wq_gate, L0_ffn_s_gate, L0_ffn_wq_up, L0_ffn_s_up, L0_ffn_wq_down, L0_ffn_s_down)
    return x

_drawn_inputs = setup_inputs


def setup_inputs(seed=0):
    import zlib

    import numpy as np

    out = dict(_drawn_inputs(seed))
    spreads = {}
    factors = {'L0_ffn_s_gate': 8.0, 'L0_ffn_s_up': 8.0, 'L0_ffn_s_down': 8.0}
    for name, (base, spread) in spreads.items():
        noise = np.random.default_rng([zlib.crc32(name.encode()), seed]).standard_normal(out[name].shape)
        drawn = base * np.exp(spread * noise) if base else spread * noise
        out[name] = jnp.asarray(drawn.astype(out[name].dtype))
    for name, factor in factors.items():
        out[name] = (out[name] * factor).astype(out[name].dtype)
    return out
```

```python
from contextlib import ExitStack

import numpy as np

import concourse.bass as bass
from concourse import mybir

F32 = mybir.dt.float32
F32R = mybir.dt.float32r
F16 = mybir.dt.float16
I32 = mybir.dt.int32
ALU = mybir.AluOpType
ACT = mybir.ActivationFunctionType
AX_X = mybir.AxisListType.X

P = 128
B, S, D = 2, 256, 512
NT = B * S // P
DC = D // P
H = 16
L = 4096
DCQ, R = 384, 64
QC = DCQ // P
CHUNK = 1024
NCH = L // CHUNK
HALF = 512
LB = L // P
TPH = S // P
NSTEP = NCH * TPH
PIECE = 256
HID = 1408
HC = HID // P
DK = D // H
HG = 4
EPS = 1e-5
ZERO_POINT = 128.0
PSCALE = 2.0 ** 14
EXP_BITS = 0x7F800000
EXP_ONE = 1 << 23
SPARE = 8


def build(nc, x, ctx_kv, wq_t, w_kcq, w_qr_t, w_kr_t, w_kckv, wo_t, cos_q, sin_q, cos_k, sin_k,
          w_mix, w_gu, w_dn, s_gu, s_dn, out):
    with ExitStack() as stack:
        def sem(name):
            return stack.enter_context(nc.semaphore(name))

        def sb(st, name, shape, dt=F32):
            return st.enter_context(nc.sbuf_tensor(name, shape, dt))

        ps_s = stack.enter_context(nc.psum_tensor("ps_s", [P, 4, HALF], F32))
        ps_t = stack.enter_context(nc.psum_tensor("ps_t", [P, 2, HALF], F32))
        ps_o = stack.enter_context(nc.psum_tensor("ps_o", [P, 2, HALF], F32))

        ident = sb(stack, "ident", [P, P])
        xres = sb(stack, "xres", [P, NT, D])
        arena = sb(stack, "arena", [P, 2 * H * B * S])
        qctx = arena[:, 0:H * B * S]
        wo_abs = arena[:, H * B * S:2 * H * B * S]
        kvr = sb(stack, "kvr", [P, B, L])
        stats = sb(stack, "stats", [P, NT, 6])
        mv = sb(stack, "mv", [P, NT, 2])
        rstd = sb(stack, "rstd", [P, NT])
        mhalf = sb(stack, "mhalf", [P, NT])
        kmax = sb(stack, "kmax", [P, H + 2])
        kexp = sb(stack, "kexp", [P, 4], I32)
        kscale = kexp[:, 2:3].bitcast(F32)
        kunscale = kexp[:, 3:4].bitcast(F32)

        with ExitStack() as st:
            xn = sb(st, "xn", [P, NT, D])
            xnT = sb(st, "xnT", [P, DC, B * S])
            wq_s = sb(st, "wq_s", [P, 2, DC, P])
            wkcq_s = sb(st, "wkcq_s", [P, 2, DCQ])
            wqr_s = sb(st, "wqr_s", [R, 2, DCQ])
            wkr_s = sb(st, "wkr_s", [R, 2, P])
            wkckv_s = sb(st, "wkckv_s", [P, 2, P])
            wot_s = sb(st, "wot_s", [P, 2, D])
            cosq = sb(st, "cosq", [P, QC, S])
            sinq = sb(st, "sinq", [P, QC, S])
            cosk = sb(st, "cosk", [P, L])
            sink = sb(st, "sink", [P, L])
            krot = sb(st, "krot", [P, B, PIECE])
            qhk = sb(st, "qhk", [P, 2, B * S])
            gmat = sb(st, "gmat", [P, 2, QC, P])
            qcos = sb(st, "qcos", [P, 2, QC, B * S])
            qrot = sb(st, "qrot", [P, 2, QC, B * S])
        with ExitStack() as st:
            kn_hi = sb(st, "kn_hi", [P, B, L], F16)
            kn_lo = sb(st, "kn_lo", [P, B, L], F16)
            kn_raw = sb(st, "kn_raw", [P, CHUNK])
            kt_hi = sb(st, "kt_hi", [P, L], F32R)
            kt_lo = sb(st, "kt_lo", [P, L], F32R)
            q_hi = sb(st, "q_hi", [P, 2, P], F32R)
            q_lo = sb(st, "q_lo", [P, 2, P], F32R)
            prob = sb(st, "prob", [P, 2, CHUNK])
            pt_hi = sb(st, "pt_hi", [P, 4, HALF], F16)
            pt_lo = sb(st, "pt_lo", [P, 4, HALF], F16)
            nmax = sb(st, "nmax", [P, 2, NCH])
            nrow = sb(st, "nrow", [P, 2, 1])
            rsum = sb(st, "rsum", [P, 2, NCH])
            alpha = sb(st, "alpha", [P, 2, NCH])
            weigh = sb(st, "weigh", [P, 2, NCH])
            junk = sb(st, "junk", [P, 2, NCH])
            lsum = sb(st, "lsum", [P, 2, 1])
            lrec = sb(st, "lrec", [P, 2, 1])
            oscl = sb(st, "oscl", [P, 2, NCH, P])
            osum = sb(st, "osum", [P, 2, P])
        with ExitStack() as st:
            ctxT = sb(st, "ctxT", [P, H, P])
            yn = sb(st, "yn", [P, 2, D])
            ynT = sb(st, "ynT", [P, 2, DC, P])
            fnT = sb(st, "fnT", [P, DC, TPH, P])
            qkv = sb(st, "qkv", [P, 2, 3, D])
            prod = sb(st, "prod", [P, 3, HG, H, DK])
            mix = sb(st, "mix", [P, H, H])
            mixo = sb(st, "mixo", [P, 2, D])
            wdn = sb(st, "wdn", [P, HC, D])
            gact = sb(st, "gact", [P, 2, S])
            hT = sb(st, "hT", [P, HC, S])
            sgu = sb(st, "sgu", [P, HC, 2])
            sdn = sb(st, "sdn", [P, D])
            dsc = sb(st, "dsc", [P, D])
            mixT = ctxT
        wmix = kvr[:, :, :].rearrange("p b c -> p (b c)")
        wgu = arena[:, 0:HC * 2 * DC * P]

        x_in = sem("x_in")
        tab_in = sem("tab_in")
        kv_in = sem("kv_in")
        wq_in = [sem(f"wq_in{i}") for i in range(2)]
        wkcq_in = [sem(f"wkcq_in{i}") for i in range(2)]
        wrest_in = [sem(f"wrest_in{i}") for i in range(2)]
        const_ok = sem("const_ok")
        st_ln = sem("st_ln")
        var_ok = sem("var_ok")
        rstd_ok = sem("rstd_ok")
        xn_ok = sem("xn_ok")
        xnT_mm = sem("xnT_mm")
        xnT_ok = sem("xnT_ok")
        a_done = sem("a_done")
        b_done = sem("b_done")
        g_done = sem("g_done")
        d_done = sem("d_done")
        c_done = sem("c_done")
        qhk_ok = sem("qhk_ok")
        g_ok = sem("g_ok")
        d_ok = sem("d_ok")
        qabs_ok = sem("qabs_ok")
        rope_mul = sem("rope_mul")
        qrope_ok = sem("qrope_ok")
        kmax_ok = sem("kmax_ok")
        kmax_all = sem("kmax_all")
        kexp_ok = sem("kexp_ok")
        krope = sem("krope")
        ktt_done = sem("ktt_done")
        kth_done = sem("kth_done")
        kt_done = sem("kt_done")
        knh_done = sem("knh_done")
        kn_done = sem("kn_done")
        s_done = sem("s_done")
        m_done = sem("m_done")
        exp_done = sem("exp_done")
        t_done = sem("t_done")
        hi_done = sem("hi_done")
        lo_done = sem("lo_done")
        pv_done = sem("pv_done")
        nrow_done = sem("nrow_done")
        al_done = sem("al_done")
        fin = sem("fin")
        o_used = sem("o_used")
        ctx_half = sem("ctx_half")
        ctx_done = sem("ctx_done")
        qh_done = sem("qh_done")
        q_ready = sem("q_ready")
        wmix_in = sem("wmix_in")
        wdn_in = sem("wdn_in")
        wgu_in = [sem(f"wgu_in{j}") for j in range(HC)]
        tr_done = sem("tr_done")
        tr_ok = sem("tr_ok")
        acc_done = sem("acc_done")
        acc_used = sem("acc_used")
        qkv_done = sem("qkv_done")
        qkv_ok = sem("qkv_ok")
        yn_ok = sem("yn_ok")
        mix_dve = sem("mix_dve")
        mix_pool = sem("mix_pool")
        mixo_ok = sem("mixo_ok")
        wdn_ok = sem("wdn_ok")
        wgu_ok = sem("wgu_ok")
        f_done = sem("f_done")
        gact_ok = sem("gact_ok")
        h_ok = sem("h_ok")
        dsc_ok = sem("dsc_ok")
        y_ok = sem("y_ok")
        y_out = sem("y_out")

        block = stack.enter_context(nc.Block())
        x_v = x.rearrange("b (u p) d -> p (b u) d", p=P)
        out_v = out.rearrange("b (u p) d -> p (b u) d", p=P)
        kv_v = ctx_kv.rearrange("b (p c) d -> p b (c d)", c=LB)
        NQT = B * H * TPH
        KN_DONE = NCH + L // PIECE - 1
        NCHUNK = NQT * NCH
        T0 = 4 * H

        @block.sync
        def _(sp):
            def load_wq(h, i):
                sp.dma_start(wq_s[:, i, :, :].rearrange("p c k -> p (c k)"),
                             wq_t[bass.ds(h, 1), :, :].rearrange("h p n -> p (h n)")).then_inc(wq_in[i], 16)

            def load_wkcq(h, i):
                sp.dma_start(wkcq_s[:, i, :],
                             w_kcq[bass.ds(h, 1), :, :].rearrange("h p n -> p (h n)")).then_inc(wkcq_in[i], 16)

            def load_rest(h, i):
                for dst, src in ((wqr_s, w_qr_t), (wkr_s, w_kr_t), (wkckv_s, w_kckv), (wot_s, wo_t)):
                    sp.dma_start(dst[:, i, :],
                                 src[bass.ds(h, 1), :, :].rearrange("h p n -> p (h n)")).then_inc(wrest_in[i], 16)

            sp.dma_start(xres[:, :, :], x_v).then_inc(x_in, 16)
            load_wq(0, 0)
            load_wkcq(0, 0)
            load_rest(0, 0)
            load_wq(1, 1)
            load_wkcq(1, 1)
            load_rest(1, 1)

            def refill(h, i):
                sp.wait_ge(a_done, h + 1)
                load_wq(h + 2, i)
                sp.wait_ge(b_done, h + 1)
                load_wkcq(h + 2, i)
                sp.wait_ge(d_done, h + 1)
                load_rest(h + 2, i)

            with sp.Fori(0, (H - 2) // 2) as pair:
                refill(2 * pair, 0)
                refill(2 * pair + 1, 1)

            sp.wait_ge(kn_done, KN_DONE)
            sp.wait_ge(kt_done, 8 * B)
            sp.dma_start(wmix, w_mix).then_inc(wmix_in, 16)
            sp.wait_ge(ctx_done, SPARE + NQT)
            sp.wait_ge(pv_done, SPARE + 2 * NCHUNK)
            sp.dma_start(wdn[:, :, :].rearrange("p c n -> p (c n)").bitcast(I32), w_dn).then_inc(wdn_in, 16)
            sp.dma_start(sgu[:, :, :].rearrange("p c n -> p (c n)"), s_gu).then_inc(wdn_in, 16)
            sp.dma_start(sdn[:, :], s_dn.partition_broadcast(P)).then_inc(wdn_in, 16)
            sp.wait_ge(acc_done, 4)
            n = 2 * DC * P
            for j in range(HC):
                sp.dma_start(wgu[:, j * n:(j + 1) * n].bitcast(I32), w_gu[:, j * n:(j + 1) * n])\
                  .then_inc(wgu_in[j], 16)
            for t in range(NT):
                sp.wait_ge(y_ok, t + 1)
                sp.dma_start(out_v[:, t, :], xres[:, t, :]).then_inc(y_out, 16)
            sp.wait_ge(y_out, 16 * NT)

        @block.gpsimd
        def _(pool):
            nc.gpsimd.memset(ident[:, :], 0.0).then_inc(const_ok, 1)
            nc.gpsimd.memset(mhalf[:, :], -0.5).then_inc(const_ok, 1)
            pool.wait_ge(const_ok, 2)
            nc.gpsimd.affine_select(out=ident[:, :], in_=ident[:, :], compare_op=ALU.not_equal, fill=1.0,
                                    base=0, pattern=[[-1, P]], channel_multiplier=1).then_inc(const_ok, 1)
            for s in (q_ready, ctx_done):
                pool.sem_inc(s, SPARE)

            def inverse_root(t0, n, done):
                pool.wait_ge(var_ok, done)
                nc.gpsimd.tensor_tensor(rstd[:, t0:t0 + n], mv[:, t0:t0 + n, 1], mhalf[:, 0:n],
                                        ALU.pow).then_inc(rstd_ok, 1)

            inverse_root(0, NT, 1)

            def q_sum(h, i):
                pool.wait_ge(rope_mul, h + 1)
                nc.gpsimd.tensor_tensor(qcos[:, i, :, :], qcos[:, i, :, :], qrot[:, i, :, :],
                                        ALU.add).then_inc(qrope_ok, 1)

            def kv_rope(h):
                at = h * PIECE
                kv = kvr[:, :, bass.ds(at, PIECE)]
                halves = kv.rearrange("p b (k a d) -> p b k a d", a=2, d=P // 2)
                rot = krot[:, :, :].rearrange("p b (k a d) -> p b k a d", a=2, d=P // 2)
                sn = sink[:, bass.ds(at, PIECE)].rearrange("p (k a d) -> p k a d", a=2, d=P // 2)
                for a in range(2):
                    nc.gpsimd.tensor_tensor(rot[:, :, :, a, :], halves[:, :, :, 1 - a, :],
                                            sn[:, :, a, :].unsqueeze(1).to_broadcast([P, B, PIECE // P, P // 2]),
                                            ALU.mult).then_inc(krope, 1)
                pool.drain()
                nc.gpsimd.tensor_tensor(kv, kv, cosk[:, bass.ds(at, PIECE)].unsqueeze(1).to_broadcast([P, B, PIECE]),
                                        ALU.mult).then_inc(krope, 1)
                pool.drain()
                nc.gpsimd.tensor_tensor(kv, kv, krot[:, :, :], ALU.add).then_inc(krope, 1)

            q_sum(0, 0)
            pool.wait_ge(kv_in, 16 * 3)
            kv_rope(0)
            with pool.Fori(0, (H - 2) // 2) as pair:
                for h, i in ((2 * pair + 1, 1), (2 * pair + 2, 0)):
                    q_sum(h, i)
                    pool.wait_ge(krope, 4 * h)
                    kv_rope(h)
            q_sum(H - 1, 1)
            pool.wait_ge(krope, 4 * (H - 1))
            kv_rope(H - 1)

            pool.wait_ge(kmax_ok, H + 1)
            nc.gpsimd.partition_all_reduce(kmax[:, H + 1:H + 2], kmax[:, H:H + 1], P,
                                           bass.bass_isa.ReduceOp.max).then_inc(kmax_all, 1)
            pool.wait_ge(krope, 4 * H)
            pool.wait_ge(c_done, H)
            pool.wait_ge(qabs_ok, H)
            pool.wait_ge(d_ok, H)

            def split_keys(b, c0, n):
                cols = bass.ds(c0, n)
                if isinstance(c0, int):
                    nc.gpsimd.tensor_scalar(kn_raw[:, 0:n], kvr[:, b, cols], kscale, None,
                                            ALU.mult).then_inc(knh_done, 1)
                else:
                    nc.gpsimd.tensor_tensor(kn_raw[:, 0:n], kvr[:, b, cols], kscale.to_broadcast([P, n]),
                                            ALU.mult).then_inc(knh_done, 1)
                pool.drain()
                nc.gpsimd.tensor_copy(kn_hi[:, b, cols], kn_raw[:, 0:n]).then_inc(knh_done, 1)
                pool.drain()
                nc.gpsimd.tensor_tensor(kn_lo[:, b, cols], kn_raw[:, 0:n], kn_hi[:, b, cols],
                                        ALU.subtract).then_inc(kn_done, 1)
                pool.drain()

            def split_query(t, i):
                pool.wait_ge(s_done, SPARE + NCH * t - NCH)
                q = qctx[:, bass.ds(t * P, P)]
                nc.gpsimd.tensor_copy(q_hi[:, i, :], q).then_inc(qh_done, 1)
                pool.drain()
                nc.gpsimd.tensor_tensor(q_lo[:, i, :], q, q_hi[:, i, :].bitcast(F32),
                                        ALU.subtract).then_inc(q_ready, 1)

            def sum_chunks(t, i):
                pool.wait_ge(o_used, SPARE + t + 1)
                nc.gpsimd.tensor_tensor(osum[:, :, :], oscl[:, i, 0:2, :], oscl[:, i, 2:4, :],
                                        ALU.add).then_inc(ctx_half, 1)
                pool.drain()
                nc.gpsimd.tensor_tensor(qctx[:, bass.ds(t * P, P)], osum[:, 0, :], osum[:, 1, :],
                                        ALU.add).then_inc(ctx_done, 1)
                pool.wait_ge(ctx_done, SPARE + t + 1)

            for b in range(B):
                t0 = b * H * TPH
                split_query(t0, 0)
                if b == 0:
                    pool.wait_ge(kexp_ok, 4)
                    for c in range(NCH):
                        split_keys(0, c * CHUNK, CHUNK)
                split_query(t0 + 1, 1)
                if b:
                    sum_chunks(t0 - 1, 1)
                split_query(t0 + 2, 0)
                sum_chunks(t0, 0)
                with pool.Fori(0, (H * TPH - 4) // 2) as pair:
                    split_query(t0 + 2 * pair + 3, 1)
                    sum_chunks(t0 + 2 * pair + 1, 1)
                    split_query(t0 + 2 * pair + 4, 0)
                    sum_chunks(t0 + 2 * pair + 2, 0)
                    if b == 0:
                        split_keys(1, pair * PIECE, PIECE)
                t = t0 + H * TPH - 3
                split_query(t + 2, 1)
                sum_chunks(t, 1)
                sum_chunks(t + 1, 0)
                if b == 0:
                    split_keys(1, L - 2 * PIECE, 2 * PIECE)
            sum_chunks(NQT - 1, 1)

            def mix_products(t):
                for n, g in enumerate((1, 3)):
                    if n == 0:
                        pool.wait_ge(qkv_ok, t + 1)
                    q = qkv[:, t % 2, 0, :].rearrange("p (h d) -> p h d", d=DK)[:, g * HG:(g + 1) * HG, :]
                    k = qkv[:, t % 2, 1, :].rearrange("p (k d) -> p k d", d=DK)
                    if t:
                        pool.wait_ge(mix_dve, MIX_STEPS * (t - 1) + MIX_FREE[g])
                    nc.gpsimd.tensor_tensor(prod[:, 1 + n], q.unsqueeze(2).to_broadcast([P, HG, H, DK]),
                                            k.unsqueeze(1).to_broadcast([P, HG, H, DK]),
                                            ALU.mult).then_inc(mix_pool, 1)
                for n, g in enumerate((1, 3)):
                    v = qkv[:, t % 2, 2, :].rearrange("p (k d) -> p d k", d=DK)
                    pool.wait_ge(mix_dve, MIX_STEPS * t + MIX_SUM[g])
                    s = mix[:, g * HG:(g + 1) * HG, :]
                    o = prod[:, 1 + n].rearrange("p h k d -> p h (k d)").rearrange("p h (d k) -> p h d k", k=H)
                    nc.gpsimd.tensor_tensor(o, s.unsqueeze(2).to_broadcast([P, HG, DK, H]),
                                            v.unsqueeze(1).to_broadcast([P, HG, DK, H]),
                                            ALU.mult).then_inc(mix_pool, 1)

            inverse_root(0, 1, 2)
            inverse_root(1, 1, 3)
            mix_products(0)
            inverse_root(2, 1, 4)
            mix_products(1)
            inverse_root(3, 1, 5)
            inverse_root(0, 1, 6)
            inverse_root(1, 1, 7)
            mix_products(2)
            mix_products(3)
            inverse_root(2, 1, 8)
            inverse_root(3, 1, 9)

        @block.scalar
        def _(act):
            act.dma_start(cosq[:, :, :].rearrange("p c s -> p (c s)"), cos_q).then_inc(tab_in, 16)
            act.dma_start(sinq[:, :, :].rearrange("p c s -> p (c s)"), sin_q).then_inc(tab_in, 16)
            act.dma_start(kvr[:, :, :], kv_v).then_inc(kv_in, 16)
            act.dma_start(cosk[:, :], cos_k).then_inc(kv_in, 16)
            act.dma_start(sink[:, :], sin_k).then_inc(kv_in, 16)
            for s in (exp_done, hi_done, al_done):
                act.sem_inc(s, SPARE)
            act.wait_ge(const_ok, 2)
            for c in range(DC):
                act.wait_ge(xnT_mm, c + 1)
                nc.scalar.copy(xnT[:, c, :], ps_s[:, c, :]).then_inc(xnT_ok, 1)

            def take_qhk(h, i):
                act.wait_ge(a_done, h + 1)
                nc.scalar.copy(qhk[:, i, :], ps_t[:, 0, :]).then_inc(qhk_ok, 1)

            def take_g_d(h, i):
                act.wait_ge(g_done, h + 1)
                nc.scalar.copy(gmat[:, i, :, :].rearrange("p c d -> p (c d)"), ps_t[:, 1, 0:DCQ]).then_inc(g_ok, 1)
                act.wait_ge(d_done, h + 1)
                nc.scalar.copy(wo_abs[:, bass.ds(h * D, D)], ps_o[:, 1, :]).then_inc(d_ok, 1)

            def take_qabs(h):
                act.wait_ge(c_done, h + 1)
                dst = qctx.rearrange("p (b c) -> p b c", b=B)[:, :, bass.ds(h * S, S)]
                nc.scalar.copy(dst, ps_o[:, 0, :].rearrange("p (b s) -> p b s", b=B)).then_inc(qabs_ok, 1)

            take_qhk(0, 0)
            take_qhk(1, 1)
            take_g_d(0, 0)
            with act.Fori(0, (H - 2) // 2) as pair:
                for h, i in ((2 * pair + 1, 1), (2 * pair + 2, 0)):
                    take_qhk(h + 1, 1 - i)
                    take_g_d(h, i)
                    take_qabs(h - 1)
            take_g_d(H - 1, 1)
            take_qabs(H - 2)
            take_qabs(H - 1)

            act.wait_ge(qrope_ok, H)
            act.wait_ge(krope, 4 * H)

            def key_columns(b):
                for g in range(8):
                    act.wait_ge(ktt_done, 8 * b + g + 1)
                    nc.scalar.copy(kt_hi[:, g * HALF:(g + 1) * HALF], ps_t[:, g % 2, :]).then_inc(kth_done, 1)

            def take_hi(u, j):
                act.wait_ge(t_done, SPARE + u + 1)
                act.wait_ge(pv_done, SPARE + u - 3)
                nc.scalar.mul(pt_hi[:, j % 4, :], ps_t[:, j % 2, :], PSCALE).then_inc(hi_done, 1)

            def exponents(n, j):
                act.wait_ge(m_done, SPARE + n + 1)
                i, c = (j // NCH) % 2, j % NCH
                nc.scalar.activation(prob[:, j % 2, :],
                                     ps_s[:, 2 * (j % 2):2 * (j % 2) + 2, :].rearrange("p a c -> p (a c)"),
                                     ACT.Exp, bias=nmax[:, i, c:c + 1], scale=1.0,
                                     accum_out=rsum[:, i, c:c + 1]).then_inc(exp_done, 1)

            def weights_of_chunks(t, i):
                act.wait_ge(nrow_done, SPARE + t + 1)
                nc.scalar.activation(alpha[:, i, :], nmax[:, i, :], ACT.Exp, bias=nrow[:, i, :],
                                     scale=-1.0).then_inc(al_done, 1)

            def head(b, h, last):
                n0 = b * H * NSTEP + h * NSTEP
                for j in range(NSTEP):
                    take_hi(2 * (n0 + j), 2 * j)
                    take_hi(2 * (n0 + j) + 1, 2 * j + 1)
                    if not (last and j == NSTEP - 1):
                        exponents(n0 + j + 1, j + 1)
                    if j % NCH == NCH - 1:
                        weights_of_chunks(b * H * TPH + h * TPH + j // NCH, j // NCH)

            for b in range(B):
                key_columns(b)
                exponents(b * H * NSTEP, 0)
                with act.Fori(0, H - 1) as h:
                    head(b, h, False)
                head(b, H - 1, True)

            def take_t(n, dst):
                act.wait_ge(tr_done, n + 1)
                nc.scalar.copy(dst, ps_t[:, n % 2, :]).then_inc(tr_ok, 1)

            def ctx_columns(t):
                for g in range(4):
                    if g == 0 and t:
                        act.wait_ge(acc_done, t)
                    take_t(BANKS.index(("ctx", t, g)), ctxT[:, 4 * g:4 * g + 4, :].rearrange("p h s -> p (h s)"))

            def take_qkv(t):
                act.wait_ge(qkv_done, t + 1)
                if t >= 2:
                    act.wait_ge(mix_dve, MIX_STEPS * (t - 1))
                nc.scalar.copy(qkv[:, t % 2, :, :], ps_s[:, 0:3, :]).then_inc(qkv_ok, 1)

            def take_xT(t):
                if t >= 2:
                    act.wait_ge(qkv_done, t - 1)
                take_t(BANKS.index(("x", t)), ynT[:, t % 2, :, :].rearrange("p c s -> p (c s)"))

            def take_mixT(t):
                if t >= 2:
                    act.wait_ge(acc_done, OUTS.index(("mix", t - 2)) + 1)
                take_t(BANKS.index(("mix", t)),
                       mixT[:, 4 * (t % 2):4 * (t % 2) + 4, :].rearrange("p h s -> p (h s)"))

            def take_fT(t):
                if t >= 2:
                    act.wait_ge(f_done, HC)
                n = BANKS.index(("f", t))
                act.wait_ge(tr_done, n + 1)
                nc.scalar.copy(fnT[:, :, t % 2, :],
                               ps_t[:, n % 2, :].rearrange("p (c s) -> p c s", c=DC)).then_inc(tr_ok, 1)

            def shift_gu(j):
                n = 2 * DC * P
                act.wait_ge(wgu_in[j], 16)
                w = wgu[:, j * n:(j + 1) * n]
                nc.scalar.activation(w, w.bitcast(I32), ACT.Copy, bias=-ZERO_POINT, scale=1.0).then_inc(wgu_ok, 1)

            def shift_down():
                act.wait_ge(wdn_in, 16 * 3)
                w = wdn[:, :, :].rearrange("p c n -> p (c n)")
                n = HC * D // 4
                for k in range(4):
                    v = w[:, k * n:(k + 1) * n]
                    nc.scalar.activation(v, v.bitcast(I32), ACT.Copy, bias=-ZERO_POINT, scale=1.0).then_inc(wdn_ok, 1)

            def silu_gate(p, j):
                n = HC * p + j
                act.wait_ge(f_done, n + 1)
                if n >= 2:
                    act.wait_ge(h_ok, n - 1)
                nc.scalar.activation(gact[:, n % 2, :], ps_s[:, n % 4, 0:S], ACT.Silu,
                                     scale=sgu[:, j, 0:1]).then_inc(gact_ok, 1)

            ctx_columns(0)
            ctx_columns(1)
            take_xT(0)
            take_qkv(0)
            ctx_columns(2)
            take_xT(1)
            take_qkv(1)
            ctx_columns(3)
            take_xT(2)
            take_qkv(2)
            shift_down()
            take_mixT(0)
            take_mixT(1)
            take_xT(3)
            take_qkv(3)
            shift_gu(0)
            shift_gu(1)
            take_fT(0)
            take_fT(1)
            for j in range(HC):
                if j + 2 < HC:
                    shift_gu(j + 2)
                silu_gate(0, j)
            take_mixT(2)
            take_mixT(3)
            take_fT(2)
            take_fT(3)
            for j in range(HC):
                silu_gate(1, j)

        @block.vector
        def _(dve):
            dve.wait_ge(x_in, 16)
            for t in range(NT):
                nc.vector.bn_stats(stats[:, t, :], xres[:, t, :]).then_inc(st_ln, 1)
            for t in range(NT):
                dve.wait_ge(st_ln, t + 1)
                nc.vector.bn_aggr(mv[:, t, :], stats[:, t, :]).then_inc(st_ln, 1)
            dve.wait_ge(st_ln, 2 * NT)
            nc.vector.tensor_scalar(mv[:, :, 1], mv[:, :, 1], EPS, None, ALU.add).then_inc(var_ok, 1)
            dve.wait_ge(rstd_ok, 1)
            for t in range(NT):
                nc.vector.tensor_scalar(xn[:, t, :], xres[:, t, :], mv[:, t, 0:1], rstd[:, t:t + 1],
                                        ALU.subtract, ALU.mult).then_inc(xn_ok, 1)
            for s in (m_done, lo_done, nrow_done, o_used):
                dve.sem_inc(s, SPARE)

            def q_rope(h, i):
                dve.wait_ge(b_done, h + 1)
                q = ps_s[:, 0:QC, :].rearrange("p c (b s) -> p c b s", b=B)
                o = qcos[:, i, :, :].rearrange("p c (b s) -> p c b s", b=B)
                nc.vector.tensor_tensor(o, q, cosq[:, :, :].unsqueeze(2).to_broadcast([P, QC, B, S]), ALU.mult)
                r = qrot[:, i, :, :].rearrange("p c (b s) -> p c b s", b=B)
                for dst, src, p0, p1 in ((0, 1, slice(0, P), slice(0, P)), (1, 0, slice(0, P), slice(0, P)),
                                         (2, 2, slice(0, P // 2), slice(P // 2, P)),
                                         (2, 2, slice(P // 2, P), slice(0, P // 2))):
                    sn = sinq[p1, dst, :]
                    last = nc.vector.tensor_tensor(r[p0, dst, :, :], q[p1, src, :, :],
                                                   sn.unsqueeze(1).to_broadcast([sn.shape[0], B, S]), ALU.mult)
                last.then_inc(rope_mul, 1)

            def largest_key(h):
                dve.wait_ge(krope, 4 * (h + 1))
                nc.vector.tensor_reduce(kmax[:, bass.ds(h, 1)], kvr[:, :, bass.ds(h * PIECE, PIECE)],
                                        mybir.AxisListType.XY, ALU.max,
                                        apply_absolute_value=True).then_inc(kmax_ok, 1)

            dve.wait_ge(tab_in, 32)
            q_rope(0, 0)
            with dve.Fori(0, (H - 2) // 2) as pair:
                for h, i in ((2 * pair + 1, 1), (2 * pair + 2, 0)):
                    q_rope(h, i)
                    largest_key(h - 1)
            q_rope(H - 1, 1)
            largest_key(H - 2)
            largest_key(H - 1)
            dve.wait_ge(kmax_ok, H)
            nc.vector.tensor_reduce(kmax[:, H:H + 1], kmax[:, 0:H], AX_X, ALU.max).then_inc(kmax_ok, 1)
            dve.wait_ge(kmax_all, 1)
            nc.vector.tensor_scalar(kexp[:, 0:1], kmax[:, H + 1:H + 2].bitcast(I32), EXP_BITS, None,
                                    ALU.bitwise_and).then_inc(kexp_ok, 1)
            dve.wait_ge(kexp_ok, 1)
            nc.vector.tensor_scalar(kexp[:, 1:2], kexp[:, 0:1], float(15 * EXP_ONE), -1.0, ALU.max,
                                    ALU.mult).then_inc(kexp_ok, 1)
            dve.wait_ge(kexp_ok, 2)
            nc.vector.tensor_scalar(kexp[:, 2:3], kexp[:, 1:2], float(268 * EXP_ONE), None,
                                    ALU.add).then_inc(kexp_ok, 1)
            nc.vector.tensor_scalar(kexp[:, 3:4], kexp[:, 1:2], -1.0, -float(14 * EXP_ONE), ALU.mult,
                                    ALU.add).then_inc(kexp_ok, 1)

            dve.wait_ge(kexp_ok, 4)
            dve.wait_ge(qrope_ok, H)
            dve.wait_ge(c_done, H)

            def key_columns(b):
                for g in range(8):
                    dve.wait_ge(kth_done, 8 * b + g + 1)
                    cols = slice(g * HALF, (g + 1) * HALF)
                    nc.vector.tensor_tensor(kt_lo[:, cols], ps_t[:, g % 2, :], kt_hi[:, cols].bitcast(F32),
                                            ALU.subtract).then_inc(kt_done, 1)

            def take_lo(u, j):
                dve.wait_ge(hi_done, SPARE + u + 1)
                nc.vector.scalar_tensor_tensor(out=pt_lo[:, j % 4, :], in0=ps_t[:, j % 2, :], scalar=PSCALE,
                                               in1=pt_hi[:, j % 4, :], op0=ALU.mult,
                                               op1=ALU.subtract).then_inc(lo_done, 1)

            def chunk_maximum(n, j):
                dve.wait_ge(s_done, SPARE + n + 1)
                i, c = (j // NCH) % 2, j % NCH
                nc.vector.tensor_reduce(nmax[:, i, c:c + 1],
                                        ps_s[:, 2 * (j % 2):2 * (j % 2) + 2, :].rearrange("p a c -> p (a c)"),
                                        AX_X, ALU.max, negate=True).then_inc(m_done, 1)

            def row_maximum(t, i):
                dve.wait_ge(m_done, SPARE + NCH * (t + 1))
                nc.vector.tensor_reduce(nrow[:, i, :], nmax[:, i, :], AX_X, ALU.min).then_inc(nrow_done, 1)

            def end_tile(t, i):
                dve.wait_ge(al_done, SPARE + t + 1)
                nc.vector.tensor_tensor_reduce(out=junk[:, i, :], in0=alpha[:, i, :], in1=rsum[:, i, :], scale=PSCALE,
                                               scalar=0.0, op0=ALU.mult, op1=ALU.add,
                                               accum_out=lsum[:, i, :]).then_inc(fin, 1)
                dve.wait_ge(fin, 3 * t + 1)
                nc.vector.reciprocal(lrec[:, i, :], lsum[:, i, :]).then_inc(fin, 1)
                dve.wait_ge(fin, 3 * t + 2)
                nc.vector.tensor_scalar(weigh[:, i, :], alpha[:, i, :], lrec[:, i, :], kunscale,
                                        ALU.mult, ALU.mult).then_inc(fin, 1)
                dve.wait_ge(fin, 3 * t + 3)
                dve.wait_ge(pv_done, SPARE + 2 * NCH * (t + 1))
                dve.wait_ge(ctx_done, SPARE + t - 1)
                nc.vector.tensor_tensor(oscl[:, i, :, :], ps_o[:, i, :].rearrange("p (c d) -> p c d", c=NCH),
                                        weigh[:, i, :].unsqueeze(2).to_broadcast([P, NCH, P]),
                                        ALU.mult).then_inc(o_used, 1)

            def head(b, h, first, last):
                n0 = b * H * NSTEP + h * NSTEP
                t0 = b * H * TPH + h * TPH
                for j in range(NSTEP):
                    take_lo(2 * (n0 + j), 2 * j)
                    take_lo(2 * (n0 + j) + 1, 2 * j + 1)
                    if j == 0 and not first:
                        end_tile(t0 - 1, 1)
                    if j == NCH:
                        end_tile(t0, 0)
                    if not (last and j >= NSTEP - 2):
                        chunk_maximum(n0 + j + 2, j + 2)
                    if j % NCH == 1:
                        row_maximum(t0 + j // NCH, j // NCH)

            for b in range(B):
                key_columns(b)
                chunk_maximum(b * H * NSTEP, 0)
                chunk_maximum(b * H * NSTEP + 1, 1)
                head(b, 0, True, False)
                with dve.Fori(1, H - 1) as h:
                    head(b, h, False, False)
                head(b, H - 1, False, True)
                end_tile((b + 1) * H * TPH - 1, 1)

            def layer_norm(k):
                kind, t = NORMS[k]
                n = OUTS.index(("out", t) if kind == "x" else ("mix", t))
                dve.wait_ge(acc_done, n + 1)
                nc.vector.tensor_tensor(xres[:, t, :], ps_o[:, n % 2, :], xres[:, t, :], ALU.add).then_inc(acc_used, 1)
                dve.wait_ge(acc_used, n + 1)
                nc.vector.bn_stats(stats[:, t, :], xres[:, t, :]).then_inc(st_ln, 1)
                dve.wait_ge(st_ln, 2 * NT + 2 * k + 1)
                nc.vector.bn_aggr(mv[:, t, :], stats[:, t, :]).then_inc(st_ln, 1)
                dve.wait_ge(st_ln, 2 * NT + 2 * k + 2)
                nc.vector.tensor_scalar(mv[:, t, 1:2], mv[:, t, 1:2], EPS, None, ALU.add).then_inc(var_ok, 1)
                dve.wait_ge(rstd_ok, 2 + k)
                if k >= 2:
                    dve.wait_ge(tr_done, max(BANKS.index(NORMS[i]) for i in range(k) if NORMS[i][1] % 2 == t % 2) + 1)
                nc.vector.tensor_scalar(yn[:, t % 2, :], xres[:, t, :], mv[:, t, 0:1], rstd[:, t:t + 1],
                                        ALU.subtract, ALU.mult).then_inc(yn_ok, 1)

            def mix_step(t, m):
                what, g = MIX_ORDER[m]
                heads = slice(g * HG, (g + 1) * HG)
                done = MIX_STEPS * t + m
                slot = 0 if g % 2 == 0 else 1 + g // 2
                by_k = prod[:, slot]
                by_d = by_k.rearrange("p h k d -> p h (k d)").rearrange("p h (d k) -> p h d k", k=H)
                if what == "mul":
                    if m == 0:
                        dve.wait_ge(qkv_ok, t + 1)
                    if done:
                        dve.wait_ge(mix_dve, done)
                    q = qkv[:, t % 2, 0, :].rearrange("p (h d) -> p h d", d=DK)[:, heads, :]
                    k = qkv[:, t % 2, 1, :].rearrange("p (k d) -> p k d", d=DK)
                    last = nc.vector.tensor_tensor(by_k, q.unsqueeze(2).to_broadcast([P, HG, H, DK]),
                                                   k.unsqueeze(1).to_broadcast([P, HG, H, DK]), ALU.mult)
                elif what == "sum":
                    if g % 2:
                        dve.wait_ge(mix_pool, 4 * t + 1 + g // 2)
                    dve.wait_ge(mix_dve, done)
                    last = nc.vector.tensor_reduce(mix[:, heads, :], by_k, AX_X, ALU.add)
                elif what == "mulv":
                    dve.wait_ge(mix_dve, done)
                    v = qkv[:, t % 2, 2, :].rearrange("p (k d) -> p d k", d=DK)
                    last = nc.vector.tensor_tensor(by_d, mix[:, heads, :].unsqueeze(2).to_broadcast([P, HG, DK, H]),
                                                   v.unsqueeze(1).to_broadcast([P, HG, DK, H]), ALU.mult)
                else:
                    if g % 2:
                        dve.wait_ge(mix_pool, 4 * t + 3 + g // 2)
                    dve.wait_ge(mix_dve, done)
                    if t >= 2:
                        dve.wait_ge(tr_done, BANKS.index(("mix", t - 2)) + 1)
                    o = mixo[:, t % 2, :].rearrange("p (h d) -> p h d", d=DK)[:, heads, :]
                    last = nc.vector.tensor_reduce(o, by_d, AX_X, ALU.add)
                last.then_inc(mix_dve, 1)

            def gate_up(p, j):
                n = HC * p + j
                dve.wait_ge(gact_ok, n + 1)
                if p:
                    dve.wait_ge(acc_done, OUTS.index(("down", TPH - 1)) + 1)
                nc.vector.scalar_tensor_tensor(out=hT[:, j, :], in0=ps_s[:, n % 4, S:2 * S], scalar=sgu[:, j, 1:2],
                                               in1=gact[:, n % 2, :], op0=ALU.mult, op1=ALU.mult).then_inc(h_ok, 1)

            def finish(t):
                n = OUTS.index(("down", t))
                dve.wait_ge(acc_done, n + 1)
                if t:
                    dve.wait_ge(y_ok, t)
                nc.vector.tensor_tensor(dsc[:, :], ps_o[:, n % 2, :], sdn[:, :], ALU.mult).then_inc(acc_used, 1)
                dve.wait_ge(acc_used, n + 1)
                nc.vector.tensor_tensor(xres[:, t, :], dsc[:, :], xres[:, t, :], ALU.add).then_inc(y_ok, 1)

            layer_norm(0)
            layer_norm(1)
            for m in range(MIX_STEPS):
                mix_step(0, m)
            layer_norm(2)
            for m in range(MIX_STEPS):
                mix_step(1, m)
            layer_norm(3)
            layer_norm(4)
            layer_norm(5)
            dve.wait_ge(wdn_in, 16 * 3)
            for m in range(2 * MIX_STEPS):
                mix_step(2 + m // MIX_STEPS, m % MIX_STEPS)
                if m % 2 and m // 2 < HC:
                    gate_up(0, m // 2)
            finish(0)
            finish(1)
            layer_norm(6)
            layer_norm(7)
            for j in range(HC):
                gate_up(1, j)
            finish(2)
            finish(3)

        @block.tensor
        def _(pe):
            for s in (s_done, t_done, pv_done):
                pe.sem_inc(s, SPARE)
            pe.wait_ge(const_ok, 3)
            pe.wait_ge(xn_ok, NT)
            for c in range(DC):
                for t in range(NT):
                    last = nc.tensor.transpose(ps_s[:, c, t * P:(t + 1) * P], xn[:, t, c * P:(c + 1) * P], ident[:, :])
                last.then_inc(xnT_mm, 1)
            pe.wait_ge(xnT_ok, DC)

            def q_head(h, i, k, first=False):
                pe.wait_ge(wq_in[i], 16 * k)
                if not first:
                    pe.wait_ge(qhk_ok, h)
                for c in range(DC):
                    last = nc.tensor.matmul(ps_t[:, 0, :], wq_s[:, i, c, :], xnT[:, c, :],
                                            start=(c == 0), stop=(c == DC - 1))
                last.then_inc(a_done, 1)

            def q_wide(h, i, k, first=False):
                pe.wait_ge(wkcq_in[i], 16 * k)
                pe.wait_ge(qhk_ok, h + 1)
                if not first:
                    pe.wait_ge(rope_mul, h)
                for c in range(QC):
                    last = nc.tensor.matmul(ps_s[:, c, :], wkcq_s[:, i, c * P:(c + 1) * P], qhk[:, i, :],
                                            start=True, stop=True)
                last.then_inc(b_done, 1)

            def fused_weights(h, i, k, first=False):
                pe.wait_ge(wrest_in[i], 64 * k)
                if not first:
                    pe.wait_ge(g_ok, h)
                for c in range(QC):
                    last = nc.tensor.matmul(ps_t[:, 1, c * P:(c + 1) * P], wqr_s[:, i, c * P:(c + 1) * P],
                                            wkr_s[:, i, :], start=True, stop=True)
                last.then_inc(g_done, 1)
                if not first:
                    pe.wait_ge(d_ok, h)
                nc.tensor.matmul(ps_o[:, 1, :], wkckv_s[:, i, :], wot_s[:, i, :],
                                 start=True, stop=True).then_inc(d_done, 1)

            def q_absorbed(h, i, first=False):
                pe.wait_ge(qrope_ok, h + 1)
                pe.wait_ge(g_ok, h + 1)
                if not first:
                    pe.wait_ge(qabs_ok, h)
                for c in range(QC):
                    last = nc.tensor.matmul(ps_o[:, 0, :], gmat[:, i, c, :], qcos[:, i, c, :],
                                            start=(c == 0), stop=(c == QC - 1))
                last.then_inc(c_done, 1)

            q_head(0, 0, 1, True)
            q_wide(0, 0, 1, True)
            q_head(1, 1, 1)
            fused_weights(0, 0, 1, True)
            q_wide(1, 1, 1)
            q_head(2, 0, 2)
            fused_weights(1, 1, 1)
            q_absorbed(0, 0, True)
            with pe.Fori(0, (H - 4) // 2) as pair:
                for h, i, k in ((2 * pair + 2, 0, pair + 2), (2 * pair + 3, 1, pair + 2)):
                    q_wide(h, i, k)
                    q_head(h + 1, 1 - i, k + i)
                    fused_weights(h, i, k)
                    q_absorbed(h - 1, 1 - i)
            q_wide(H - 2, 0, H // 2)
            q_head(H - 1, 1, H // 2)
            fused_weights(H - 2, 0, H // 2)
            q_absorbed(H - 3, 1)
            q_wide(H - 1, 1, H // 2)
            fused_weights(H - 1, 1, H // 2)
            q_absorbed(H - 2, 0)
            q_absorbed(H - 1, 1)

            pe.wait_ge(krope, 4 * H)
            pe.wait_ge(qhk_ok, H)
            pe.wait_ge(g_ok, H)
            pe.wait_ge(rope_mul, H)
            pe.wait_ge(d_ok, H)
            pe.wait_ge(qabs_ok, H)

            def key_columns(b):
                for g in range(8):
                    if b and g < 2:
                        pe.wait_ge(lo_done, SPARE + 2 * b * H * NSTEP)
                    if g >= 2:
                        pe.wait_ge(kt_done, 8 * b + g - 1)
                    for k in range(4):
                        blk = 4 * g + k
                        last = nc.tensor.transpose(ps_t[:, g % 2, k * P:(k + 1) * P],
                                                   kvr[:, b, blk * P:(blk + 1) * P], ident[:, :])
                    last.then_inc(ktt_done, 1)
                pe.wait_ge(kt_done, 8 * (b + 1))

            def transposes(n, j):
                pe.wait_ge(exp_done, SPARE + n + 1)
                for u in range(2):
                    pe.wait_ge(lo_done, SPARE + 2 * n + u - 1)
                    for k in range(4):
                        c0 = (4 * u + k) * P
                        last = nc.tensor.transpose(ps_t[:, u, k * P:(k + 1) * P], prob[:, j % 2, c0:c0 + P],
                                                   ident[:, :])
                    last.then_inc(t_done, 1)

            def scores(j):
                i, c = (j // NCH) % 2, j % NCH
                for a in range(2):
                    o = ps_s[:, 2 * (j % 2) + a, :]
                    cols = slice(c * CHUNK + a * HALF, c * CHUNK + (a + 1) * HALF)
                    nc.tensor.matmul(o, q_hi[:, i, :], kt_hi[:, cols], start=True, stop=False)
                    nc.tensor.matmul(o, q_hi[:, i, :], kt_lo[:, cols], start=False, stop=False)
                    last = nc.tensor.matmul(o, q_lo[:, i, :], kt_hi[:, cols], start=False, stop=True)
                last.then_inc(s_done, 1)

            def weighed_keys(b, n, t, j):
                i, c = (j // NCH) % 2, j % NCH
                if c == 0:
                    pe.wait_ge(o_used, SPARE + t - 1)
                o = ps_o[:, i, c * P:(c + 1) * P]
                for u in range(2):
                    pe.wait_ge(lo_done, SPARE + 2 * n + u + 1)
                    for k in range(4):
                        blk = c * (CHUNK // P) + 4 * u + k
                        hi = pt_hi[:, (2 * j + u) % 4, k * P:(k + 1) * P]
                        lo = pt_lo[:, (2 * j + u) % 4, k * P:(k + 1) * P]
                        v_hi = kn_hi[:, b, blk * P:(blk + 1) * P]
                        v_lo = kn_lo[:, b, blk * P:(blk + 1) * P]
                        nc.tensor.matmul(o, hi, v_hi, start=(u == 0 and k == 0), stop=False)
                        nc.tensor.matmul(o, hi, v_lo, start=False, stop=False)
                        last = nc.tensor.matmul(o, lo, v_hi, start=False, stop=(u == 1 and k == 3))
                    last.then_inc(pv_done, 1)

            def head(b, h, first, last):
                n0 = b * H * NSTEP + h * NSTEP
                t0 = b * H * TPH + h * TPH
                for j in range(NSTEP):
                    transposes(n0 + j, j)
                    if not (last and j >= NSTEP - 2):
                        if (j + 2) % NCH == 0:
                            pe.wait_ge(q_ready, SPARE + t0 + (j + 2) // NCH + 1)
                        scores(j + 2)
                    if first and j < NCH:
                        pe.wait_ge(kn_done, j + 1 if b == 0 else KN_DONE)
                    weighed_keys(b, n0 + j, t0 + j // NCH, j)

            for b in range(B):
                key_columns(b)
                pe.wait_ge(q_ready, SPARE + b * H * TPH + 1)
                if b:
                    pe.wait_ge(exp_done, SPARE + b * H * NSTEP)
                scores(0)
                scores(1)
                head(b, 0, True, False)
                with pe.Fori(1, H - 1) as h:
                    head(b, h, False, False)
                head(b, H - 1, False, True)

            def turn(bank, src, ready, count):
                n = BANKS.index(bank)
                pe.wait_ge(ready, count)
                if n >= 2:
                    pe.wait_ge(tr_ok, n - 1)
                for k in range(4):
                    last = nc.tensor.transpose(ps_t[:, n % 2, k * P:(k + 1) * P], src(k), ident[:, :])
                last.then_inc(tr_done, 1)

            def ready_out(n):
                if n >= 2:
                    pe.wait_ge(acc_used, n - 1)
                return ps_o[:, n % 2, :]

            def context_out(t):
                for g in range(4):
                    turn(("ctx", t, g), lambda k: qctx[:, ctx_tile(t, 4 * g + k):ctx_tile(t, 4 * g + k) + P],
                         ctx_done, SPARE + NQT)
                pe.wait_ge(tr_ok, BANKS.index(("ctx", t, 3)) + 1)
                o = ready_out(OUTS.index(("out", t)))
                for h in range(H):
                    last = nc.tensor.matmul(o, ctxT[:, h, :], wo_abs[:, h * D:(h + 1) * D],
                                            start=(h == 0), stop=(h == H - 1))
                last.then_inc(acc_done, 1)

            def turn_norm(k):
                kind, t = NORMS[k]
                turn((kind, t), lambda c: yn[:, t % 2, c * P:(c + 1) * P], yn_ok, k + 1)

            def mix_in(t):
                pe.wait_ge(tr_ok, BANKS.index(("x", t)) + 1)
                pe.wait_ge(wmix_in, 16)
                if t:
                    pe.wait_ge(qkv_ok, t)
                for m in range(3):
                    for c in range(DC):
                        last = nc.tensor.matmul(ps_s[:, m, :], ynT[:, t % 2, c, :],
                                                wmix[:, (m * DC + c) * D:(m * DC + c + 1) * D],
                                                start=(c == 0), stop=(c == DC - 1))
                last.then_inc(qkv_done, 1)

            def mix_out(t):
                turn(("mix", t), lambda c: mixo[:, t % 2, c * P:(c + 1) * P], mix_dve, MIX_STEPS * (t + 1))
                pe.wait_ge(tr_ok, BANKS.index(("mix", t)) + 1)
                o = ready_out(OUTS.index(("mix", t)))
                for c in range(DC):
                    last = nc.tensor.matmul(o, mixT[:, 4 * (t % 2) + c, :],
                                            wmix[:, (3 * DC + c) * D:(3 * DC + c + 1) * D],
                                            start=(c == 0), stop=(c == DC - 1))
                last.then_inc(acc_done, 1)

            def gate_up(p):
                pe.wait_ge(tr_ok, BANKS.index(("f", 2 * p + 1)) + 1)
                for j in range(HC):
                    n = HC * p + j
                    pe.wait_ge(wgu_ok, j + 1)
                    if n >= 4:
                        pe.wait_ge(h_ok, n - 3)
                    else:
                        pe.wait_ge(qkv_ok, NT)
                    for m in range(2):
                        for c in range(DC):
                            w = wgu[:, ((2 * j + m) * DC + c) * P:((2 * j + m) * DC + c + 1) * P]
                            last = nc.tensor.matmul(ps_s[:, n % 4, m * S:(m + 1) * S], w,
                                                    fnT[:, c, :, :].rearrange("p u s -> p (u s)"),
                                                    start=(c == 0), stop=(c == DC - 1))
                    last.then_inc(f_done, 1)

            def down(t):
                pe.wait_ge(h_ok, HC * (t // TPH + 1))
                pe.wait_ge(wdn_ok, 4)
                o = ready_out(OUTS.index(("down", t)))
                for j in range(HC):
                    last = nc.tensor.matmul(o, hT[:, j, (t % TPH) * P:(t % TPH + 1) * P], wdn[:, j, :],
                                            start=(j == 0), stop=(j == HC - 1))
                last.then_inc(acc_done, 1)

            context_out(0)
            context_out(1)
            turn_norm(0)
            mix_in(0)
            context_out(2)
            turn_norm(1)
            mix_in(1)
            context_out(3)
            turn_norm(2)
            mix_in(2)
            mix_out(0)
            mix_out(1)
            turn_norm(3)
            mix_in(3)
            turn_norm(4)
            turn_norm(5)
            gate_up(0)
            down(0)
            down(1)
            mix_out(2)
            mix_out(3)
            turn_norm(6)
            turn_norm(7)
            gate_up(1)
            down(2)
            down(3)


MIX_ORDER = [("mul", 0), ("sum", 0), ("mul", 2), ("sum", 2), ("sum", 1), ("sum", 3),
             ("mulv", 0), ("sumv", 0), ("mulv", 2), ("sumv", 2), ("sumv", 1), ("sumv", 3)]
MIX_STEPS = len(MIX_ORDER)
MIX_SUM = {g: MIX_ORDER.index(("sum", g)) + 1 for g in range(4)}
MIX_FREE = {g: MIX_ORDER.index(("sumv", g)) + 1 for g in range(4)}
BANKS = ([("ctx", 0, g) for g in range(4)] + [("ctx", 1, g) for g in range(4)] + [("x", 0)]
         + [("ctx", 2, g) for g in range(4)] + [("x", 1)] + [("ctx", 3, g) for g in range(4)]
         + [("x", 2), ("mix", 0), ("mix", 1), ("x", 3), ("f", 0), ("f", 1),
            ("mix", 2), ("mix", 3), ("f", 2), ("f", 3)])
OUTS = [("out", 0), ("out", 1), ("out", 2), ("out", 3), ("mix", 0), ("mix", 1), ("down", 0), ("down", 1),
        ("mix", 2), ("mix", 3), ("down", 2), ("down", 3)]
NORMS = [("x", 0), ("x", 1), ("x", 2), ("x", 3), ("f", 0), ("f", 1), ("f", 2), ("f", 3)]


def ctx_tile(t, h):
    return ((t // TPH * H + h) * TPH + t % TPH) * P


def rope_tables(length, dim):
    inv = (np.float32(1.0) / np.power(np.float32(10000.0), np.arange(0, dim, 2, dtype=np.float32)
                                      / np.float32(dim)).astype(np.float32)).astype(np.float32)
    f = (np.arange(length, dtype=np.float32)[:, None] * inv[None, :]).astype(np.float32)
    sin = np.repeat(np.sin(f), 2, axis=-1).astype(np.float32)
    cos = np.repeat(np.cos(f), 2, axis=-1).astype(np.float32)
    sin[:, :dim // 2] *= -1
    return sin, cos


def kernel(x, ctx_512, L0_xattn_Wq, L0_xattn_w_kc_q, L0_xattn_w_kc_kv, L0_xattn_W_qr, L0_xattn_W_kr,
           L0_xattn_Wo, L0_attn_Wq, L0_attn_Wk, L0_attn_Wv, L0_attn_Wo, L0_ffn_wq_gate, L0_ffn_s_gate,
           L0_ffn_wq_up, L0_ffn_s_up, L0_ffn_wq_down, L0_ffn_s_down):
    import concourse.bacc as bacc
    from concourse.bass_utils import run_bass_kernel_spmd

    half = DCQ // 2
    perm = np.concatenate([np.arange(0, P), np.arange(half, half + P), np.arange(P, half),
                           np.arange(half + P, DCQ)])
    sin, cos = rope_tables(S, DCQ)
    cos_q = cos.T[perm].reshape(QC, P, S).transpose(1, 0, 2).reshape(P, QC * S)
    sq = sin.T[perm].reshape(QC, P, S)
    sq = np.stack([sq[0], sq[1], np.concatenate([sq[2, P // 2:], sq[2, :P // 2]])])
    sin_q = sq.transpose(1, 0, 2).reshape(P, QC * S)
    sin, cos = rope_tables(L, P)
    gate = np.asarray(L0_ffn_wq_gate).T.reshape(DC, P, HC, P)
    up = np.asarray(L0_ffn_wq_up).T.reshape(DC, P, HC, P)
    ins = {
        "x": x,
        "ctx_kv": ctx_512,
        "wq_t": np.asarray(L0_xattn_Wq).reshape(H, P, DC, P).transpose(0, 3, 2, 1).reshape(H, P, DC * P),
        "w_kcq": np.asarray(L0_xattn_w_kc_q)[:, :, perm],
        "w_qr_t": np.asarray(L0_xattn_W_qr)[:, perm, :].transpose(0, 2, 1),
        "w_kr_t": np.asarray(L0_xattn_W_kr).transpose(0, 2, 1),
        "w_kckv": L0_xattn_w_kc_kv,
        "wo_t": np.asarray(L0_xattn_Wo).T.reshape(H, P, D),
        "cos_q": cos_q,
        "sin_q": sin_q,
        "cos_k": cos.reshape(P, L),
        "sin_k": sin.reshape(P, L),
        "w_mix": np.concatenate([np.asarray(w).reshape(DC, P, D).transpose(1, 0, 2).reshape(P, DC * D)
                                 for w in (L0_attn_Wq, L0_attn_Wk, L0_attn_Wv, L0_attn_Wo)], axis=1),
        "w_gu": np.stack([gate, up]).transpose(2, 3, 0, 1, 4).reshape(P, HC * 2 * DC * P),
        "w_dn": np.asarray(L0_ffn_wq_down).T.reshape(HC, P, D).transpose(1, 0, 2).reshape(P, HC * D),
        "s_gu": np.stack([np.asarray(L0_ffn_s_gate), np.asarray(L0_ffn_s_up)], axis=-1)
                  .reshape(HC, P, 2).transpose(1, 0, 2).reshape(P, HC * 2),
        "s_dn": L0_ffn_s_down,
    }
    nc = bacc.Bacc("TRN2", target_bir_lowering=False, num_devices=1)
    arrays, aps = {}, {}
    for name, a in ins.items():
        a = np.ascontiguousarray(a)
        arrays[f"{name}_dram"] = a
        aps[name] = nc.dram_tensor(f"{name}_dram", list(a.shape), mybir.dt.from_np(a.dtype), kind="ExternalInput").ap()
    out = nc.dram_tensor("out_dram", [B, S, D], F32, kind="ExternalOutput").ap()
    build(nc, out=out, **aps)
    r = run_bass_kernel_spmd(nc, [arrays], core_ids=[0])
    return r.results[0]["out_dram"]
```

```python
from contextlib import ExitStack

import numpy as np

import concourse.bass as bass
from concourse import mybir

F32 = mybir.dt.float32
F32R = mybir.dt.float32r
F16 = mybir.dt.float16
I32 = mybir.dt.int32
ALU = mybir.AluOpType
ACT = mybir.ActivationFunctionType
AX_X = mybir.AxisListType.X

P = 128
B, S, D = 2, 256, 512
NT = B * S // P
DC = D // P
H = 16
L = 4096
DCQ, R = 384, 64
QC = DCQ // P
CHUNK = 1024
NCH = L // CHUNK
HALF = 512
LB = L // P
TPH = S // P
NSTEP = NCH * TPH
PIECE = 512
NP = L // PIECE
HID = 1408
HC = HID // P
DK = D // H
HG = 4
EPS = 1e-5
ZERO_POINT = 128.0
PSCALE = 2.0 ** 14
EXP_BITS = 0x7F800000
EXP_ONE = 1 << 23
AHEAD = 4
SPARE = 8


def build(nc, x, ctx_kv, wq_t, w_kcq, w_qr_t, w_kr_t, w_kckv, wo_t, cos_q, sin_q, cos_k, sin_k,
          w_mix, w_gu, w_dn, s_gu, s_dn, out):
    with ExitStack() as stack:
        def sem(name):
            return stack.enter_context(nc.semaphore(name))

        def sb(st, name, shape, dt=F32):
            return st.enter_context(nc.sbuf_tensor(name, shape, dt))

        ps_s = stack.enter_context(nc.psum_tensor("ps_s", [P, 4, HALF], F32))
        ps_t = stack.enter_context(nc.psum_tensor("ps_t", [P, 2, HALF], F32))
        ps_o = stack.enter_context(nc.psum_tensor("ps_o", [P, 2, HALF], F32))

        ident = sb(stack, "ident", [P, P])
        arena = sb(stack, "arena", [P, 2 * H * B * S])
        qctx = arena[:, 0:H * B * S]
        wo_abs = arena[:, H * B * S:2 * H * B * S]
        kvr = sb(stack, "kvr", [P, B, L])
        stats = sb(stack, "stats", [P, NT, 6])
        mv = sb(stack, "mv", [P, NT, 2])
        rstd = sb(stack, "rstd", [P, NT])
        mhalf = sb(stack, "mhalf", [P, NT])
        kmax = sb(stack, "kmax", [P, NP + 2])
        kexp = sb(stack, "kexp", [P, 4], I32)
        kscale = kexp[:, 2:3].bitcast(F32)
        kunscale = kexp[:, 3:4].bitcast(F32)
        with ExitStack() as keys:
            kn0_hi = sb(keys, "kn0_hi", [P, L], F16)
            kn0_lo = sb(keys, "kn0_lo", [P, L], F16)
            kn_raw = sb(keys, "kn_raw", [P, PIECE])
            with ExitStack() as st:
                x_in1 = sb(st, "x_in1", [P, NT, D])
                cs_k = sb(st, "cs_k", [P, 2, 2, PIECE])
                krot = sb(st, "krot", [P, B, PIECE])
                xnT = sb(st, "xnT", [P, DC, B * S])
                wq_s = sb(st, "wq_s", [P, 2, DC, P])
                wkcq_s = sb(st, "wkcq_s", [P, 2, DCQ])
                wqr_s = sb(st, "wqr_s", [R, 2, DCQ])
                wkr_s = sb(st, "wkr_s", [R, 2, P])
                wkckv_s = sb(st, "wkckv_s", [P, 2, P])
                wot_s = sb(st, "wot_s", [P, 2, D])
                cosq = sb(st, "cosq", [P, QC, S])
                sinq = sb(st, "sinq", [P, QC, S])
                qhk = sb(st, "qhk", [P, 2, B * S])
                gmat = sb(st, "gmat", [P, 2, QC, P])
                qcos = sb(st, "qcos", [P, 2, QC, B * S])
                qrot = sb(st, "qrot", [P, 2, QC, B * S])
                xn = qrot[:, :, :, :].rearrange("p i c s -> p (i c s)")[:, 0:NT * D]\
                    .rearrange("p (t d) -> p t d", d=D)
            with ExitStack() as st:
                kt_hi = sb(st, "kt_hi", [P, L], F32R)
                kt_lo = sb(st, "kt_lo", [P, L], F32R)
                q_hi = sb(st, "q_hi", [P, 2, P], F32R)
                q_lo = sb(st, "q_lo", [P, 2, P], F32R)
                prob = sb(st, "prob", [P, 2, CHUNK])
                p_hi = sb(st, "p_hi", [P, 2, CHUNK], F16)
                p_lo = sb(st, "p_lo", [P, 2, CHUNK], F16)
                pt_hi = sb(st, "pt_hi", [P, 4, CHUNK // P, P], F16)
                pt_lo = sb(st, "pt_lo", [P, 4, CHUNK // P, P], F16)
                nmax = sb(st, "nmax", [P, 2, NCH])
                nrow = sb(st, "nrow", [P, 2, 1])
                rsum = sb(st, "rsum", [P, 2, NCH])
                alpha = sb(st, "alpha", [P, 2, NCH])
                weigh = sb(st, "weigh", [P, 2, NCH])
                junk = sb(st, "junk", [P, 2, NCH])
                lsum = sb(st, "lsum", [P, 2, 1])
                lrec = sb(st, "lrec", [P, 2, 1])
                oscl = sb(st, "oscl", [P, 2, NCH, P])
                osum = sb(st, "osum", [P, 2, P])
                kn1_hi = sb(st, "kn1_hi", [P, L], F16)
                kn1_lo = sb(st, "kn1_lo", [P, L], F16)
        with ExitStack() as st:
            xres = sb(st, "xres", [P, NT, D])
            ctxT = sb(st, "ctxT", [P, H, P])
            yn = sb(st, "yn", [P, 2, D])
            ynT = sb(st, "ynT", [P, 2, DC, P])
            fnT = sb(st, "fnT", [P, DC, TPH, P])
            qkv = sb(st, "qkv", [P, 2, 3, D])
            prod = sb(st, "prod", [P, 3, HG, H, DK])
            mix = sb(st, "mix", [P, H, H])
            mixo = sb(st, "mixo", [P, 2, D])
            wdn = sb(st, "wdn", [P, HC, D])
            gact = sb(st, "gact", [P, 2, S])
            hT = sb(st, "hT", [P, HC, S])
            sgu = sb(st, "sgu", [P, HC, 2])
            sdn = sb(st, "sdn", [P, D])
            dsc = sb(st, "dsc", [P, D])
            mixT = ctxT
        kn_hi, kn_lo = (kn0_hi, kn1_hi), (kn0_lo, kn1_lo)
        wmix = kvr[:, :, :].rearrange("p b c -> p (b c)")
        wgu = arena[:, 0:HC * 2 * DC * P]

        x_in = sem("x_in")
        x_again = sem("x_again")
        tab_in = sem("tab_in")
        kv_in = [sem(f"kv_in{i}") for i in range(4)]
        cs_in = [sem(f"cs_in{i}") for i in range(2)]
        wq_in = [sem(f"wq_in{i}") for i in range(2)]
        wkcq_in = [sem(f"wkcq_in{i}") for i in range(2)]
        wrest_in = [sem(f"wrest_in{i}") for i in range(2)]
        const_ok = sem("const_ok")
        st_ln = sem("st_ln")
        var_ok = sem("var_ok")
        rstd_ok = sem("rstd_ok")
        xn_ok = sem("xn_ok")
        xnT_mm = sem("xnT_mm")
        xnT_ok = sem("xnT_ok")
        a_done = sem("a_done")
        b_done = sem("b_done")
        g_done = sem("g_done")
        d_done = sem("d_done")
        c_done = sem("c_done")
        qhk_ok = sem("qhk_ok")
        g_ok = sem("g_ok")
        d_ok = sem("d_ok")
        qabs_ok = sem("qabs_ok")
        rope_mul = sem("rope_mul")
        qrope_ok = sem("qrope_ok")
        kmax_ok = sem("kmax_ok")
        kmax_all = sem("kmax_all")
        kexp_ok = sem("kexp_ok")
        krope = sem("krope")
        ktt_done = sem("ktt_done")
        kth_done = sem("kth_done")
        kt_done = sem("kt_done")
        knh_done = sem("knh_done")
        kn_done = sem("kn_done")
        s_done = sem("s_done")
        m_done = sem("m_done")
        exp_done = sem("exp_done")
        turn_go = sem("turn_go")
        hi_in = [sem(f"hi_in{i}") for i in range(2)]
        lo_in = [sem(f"lo_in{i}") for i in range(2)]
        hi_done = sem("hi_done")
        lo_done = sem("lo_done")
        pv_done = sem("pv_done")
        nrow_done = sem("nrow_done")
        al_done = sem("al_done")
        fin = sem("fin")
        o_used = sem("o_used")
        ctx_half = sem("ctx_half")
        ctx_done = sem("ctx_done")
        qh_done = sem("qh_done")
        q_ready = sem("q_ready")
        wmix_in = sem("wmix_in")
        wdn_in = sem("wdn_in")
        wgu_in = [sem(f"wgu_in{j}") for j in range(HC)]
        tr_done = sem("tr_done")
        tr_ok = sem("tr_ok")
        acc_done = sem("acc_done")
        acc_used = sem("acc_used")
        qkv_done = sem("qkv_done")
        qkv_ok = sem("qkv_ok")
        yn_ok = sem("yn_ok")
        mix_dve = sem("mix_dve")
        mix_pool = sem("mix_pool")
        mixo_ok = sem("mixo_ok")
        wdn_ok = sem("wdn_ok")
        wgu_ok = sem("wgu_ok")
        f_done = sem("f_done")
        gact_ok = sem("gact_ok")
        h_ok = sem("h_ok")
        dsc_ok = sem("dsc_ok")
        y_ok = sem("y_ok")
        y_out = sem("y_out")

        block = stack.enter_context(nc.Block())
        x_v = x.rearrange("b (u p) d -> p (b u) d", p=P)
        out_v = out.rearrange("b (u p) d -> p (b u) d", p=P)
        kv_v = ctx_kv.rearrange("b (p c) d -> p b (c d)", c=LB)
        NQT = B * H * TPH
        KN_DONE = B * NP
        NCHUNK = NQT * NCH
        T0 = 4 * H

        @block.sync
        def _(sp):
            def load_wq(h, i):
                sp.dma_start(wq_s[:, i, :, :].rearrange("p c k -> p (c k)"),
                             wq_t[bass.ds(h, 1), :, :].rearrange("h p n -> p (h n)")).then_inc(wq_in[i], 16)

            def load_wkcq(h, i):
                sp.dma_start(wkcq_s[:, i, :],
                             w_kcq[bass.ds(h, 1), :, :].rearrange("h p n -> p (h n)")).then_inc(wkcq_in[i], 16)

            def load_rest(h, i):
                for dst, src in ((wqr_s, w_qr_t), (wkr_s, w_kr_t), (wkckv_s, w_kckv), (wot_s, wo_t)):
                    sp.dma_start(dst[:, i, :],
                                 src[bass.ds(h, 1), :, :].rearrange("h p n -> p (h n)")).then_inc(wrest_in[i], 16)

            def load_turn(p, i):
                for m, src in ((0, cos_k), (1, sin_k)):
                    sp.dma_start(cs_k[:, i, m, :], src[:, bass.ds(p * PIECE, PIECE)]).then_inc(cs_in[i], 16)

            sp.dma_start(x_in1[:, :, :], x_v).then_inc(x_in, 16)
            load_wq(0, 0)
            load_wkcq(0, 0)
            sp.dma_start(cosq[:, :, :].rearrange("p c s -> p (c s)"), cos_q).then_inc(tab_in, 16)
            sp.dma_start(sinq[:, :, :].rearrange("p c s -> p (c s)"), sin_q).then_inc(tab_in, 16)
            load_rest(0, 0)
            load_turn(0, 0)
            load_wq(1, 1)
            load_wkcq(1, 1)
            load_rest(1, 1)
            load_turn(1, 1)

            def refill(h, i):
                sp.wait_ge(a_done, h + 1)
                load_wq(h + 2, i)
                sp.wait_ge(b_done, h + 1)
                load_wkcq(h + 2, i)
                sp.wait_ge(d_done, h + 1)
                load_rest(h + 2, i)

            with sp.Fori(0, (NP - 2) // 2) as pair:
                for h, i in ((2 * pair, 0), (2 * pair + 1, 1)):
                    refill(h, i)
                    sp.wait_ge(krope, 4 * (h + 1))
                    load_turn(h + 2, i)
            with sp.Fori((NP - 2) // 2, (H - 2) // 2) as pair:
                refill(2 * pair, 0)
                refill(2 * pair + 1, 1)

            def turn_exponents(b, h, j):
                n = b * H * NSTEP + h * NSTEP + j
                sp.wait_ge(pv_done, SPARE + n - 3)
                sp.sem_inc(turn_go, 1)
                sp.wait_ge(hi_done, SPARE + n + 1)
                sp.sem_inc(turn_go, 1)
                sp.dma_start(pt_hi[:, j % 4], p_hi[:, j % 2, :], transpose=True).then_inc(hi_in[j % 2], 16)
                sp.wait_ge(lo_done, SPARE + n + 1)
                sp.sem_inc(turn_go, 1)
                sp.dma_start(pt_lo[:, j % 4], p_lo[:, j % 2, :], transpose=True).then_inc(lo_in[j % 2], 16)

            for b in range(B):
                if b == B - 1:
                    sp.wait_ge(kt_done, 8 * B)
                with sp.Fori(0, H) as h:
                    for j in range(NSTEP):
                        turn_exponents(b, h, j)
                    if b == B - 1:
                        sp.wait_ge(kn_done, KN_DONE)
                        sp.dma_start(wmix[:, bass.ts(h, D)], w_mix[:, bass.ts(h, D)]).then_inc(wmix_in, 16)

            sp.wait_ge(pv_done, SPARE + NCHUNK // B)
            sp.dma_start(xres[:, :, :], x_v).then_inc(x_again, 16)
            sp.wait_ge(ctx_done, SPARE + NQT)
            sp.wait_ge(pv_done, SPARE + NCHUNK)
            sp.dma_start(wdn[:, :, :].rearrange("p c n -> p (c n)").bitcast(I32), w_dn).then_inc(wdn_in, 16)
            sp.dma_start(sgu[:, :, :].rearrange("p c n -> p (c n)"), s_gu).then_inc(wdn_in, 16)
            sp.dma_start(sdn[:, :], s_dn.partition_broadcast(P)).then_inc(wdn_in, 16)
            sp.wait_ge(acc_done, 4)
            n = 2 * DC * P
            for j in range(HC):
                sp.dma_start(wgu[:, j * n:(j + 1) * n].bitcast(I32), w_gu[:, j * n:(j + 1) * n])\
                  .then_inc(wgu_in[j], 16)
            for t in range(NT):
                sp.wait_ge(y_ok, t + 1)
                sp.dma_start(out_v[:, t, :], xres[:, t, :]).then_inc(y_out, 16)
            sp.wait_ge(y_out, 16 * NT)

        @block.gpsimd
        def _(pool):
            nc.gpsimd.memset(ident[:, :], 0.0).then_inc(const_ok, 1)
            nc.gpsimd.memset(mhalf[:, :], -0.5).then_inc(const_ok, 1)
            pool.wait_ge(const_ok, 2)
            nc.gpsimd.affine_select(out=ident[:, :], in_=ident[:, :], compare_op=ALU.not_equal, fill=1.0,
                                    base=0, pattern=[[-1, P]], channel_multiplier=1).then_inc(const_ok, 1)
            for s in (q_ready, ctx_done):
                pool.sem_inc(s, SPARE)

            def inverse_root(t0, n, done):
                pool.wait_ge(var_ok, done)
                nc.gpsimd.tensor_tensor(rstd[:, t0:t0 + n], mv[:, t0:t0 + n, 1], mhalf[:, 0:n],
                                        ALU.pow).then_inc(rstd_ok, 1)

            inverse_root(0, NT, 1)

            def kv_rope(p, i, k):
                pool.wait_ge(cs_in[i], 32 * k)
                kv = kvr[:, :, bass.ds(p * PIECE, PIECE)]
                halves = kv.rearrange("p b (k a d) -> p b k a d", a=2, d=P // 2)
                rot = krot[:, :, :].rearrange("p b (k a d) -> p b k a d", a=2, d=P // 2)
                sn = cs_k[:, i, 1, :].rearrange("p (k a d) -> p k a d", a=2, d=P // 2)
                for a in range(2):
                    nc.gpsimd.tensor_tensor(rot[:, :, :, a, :], halves[:, :, :, 1 - a, :],
                                            sn[:, :, a, :].unsqueeze(1).to_broadcast([P, B, PIECE // P, P // 2]),
                                            ALU.mult).then_inc(krope, 1)
                pool.drain()
                nc.gpsimd.tensor_tensor(kv, kv, cs_k[:, i, 0, :].unsqueeze(1).to_broadcast([P, B, PIECE]),
                                        ALU.mult).then_inc(krope, 1)
                pool.drain()
                nc.gpsimd.tensor_tensor(kv, kv, krot[:, :, :], ALU.add).then_inc(krope, 1)
                pool.drain()

            with pool.Fori(0, NP // 2) as pair:
                for q in range(4):
                    pool.wait_ge(kv_in[q], 16)
                kv_rope(2 * pair, 0, pair + 1)
                kv_rope(2 * pair + 1, 1, pair + 1)
            pool.wait_ge(kmax_ok, NP + 1)
            nc.gpsimd.partition_all_reduce(kmax[:, NP + 1:NP + 2], kmax[:, NP:NP + 1], P,
                                           bass.bass_isa.ReduceOp.max).then_inc(kmax_all, 1)

            def split_keys(b, p):
                cols = bass.ds(p * PIECE, PIECE)
                nc.gpsimd.tensor_tensor(kn_raw[:, :], kvr[:, b, cols], kscale.to_broadcast([P, PIECE]),
                                        ALU.mult).then_inc(knh_done, 1)
                pool.drain()
                nc.gpsimd.tensor_copy(kn_hi[b][:, cols], kn_raw[:, :]).then_inc(knh_done, 1)
                pool.drain()
                nc.gpsimd.tensor_tensor(kn_lo[b][:, cols], kn_raw[:, :], kn_hi[b][:, cols],
                                        ALU.subtract).then_inc(kn_done, 1)
                pool.drain()

            def split_query(t, i):
                pool.wait_ge(s_done, SPARE + NCH * t - NCH)
                q = qctx[:, bass.ds(t * P, P)]
                nc.gpsimd.tensor_copy(q_hi[:, i, :], q).then_inc(qh_done, 1)
                pool.drain()
                nc.gpsimd.tensor_tensor(q_lo[:, i, :], q, q_hi[:, i, :].bitcast(F32),
                                        ALU.subtract).then_inc(q_ready, 1)

            def sum_chunks(t, i):
                pool.wait_ge(o_used, SPARE + t + 1)
                nc.gpsimd.tensor_tensor(osum[:, :, :], oscl[:, i, 0:2, :], oscl[:, i, 2:4, :],
                                        ALU.add).then_inc(ctx_half, 1)
                pool.drain()
                nc.gpsimd.tensor_tensor(qctx[:, bass.ds(t * P, P)], osum[:, 0, :], osum[:, 1, :],
                                        ALU.add).then_inc(ctx_done, 1)
                pool.wait_ge(ctx_done, SPARE + t + 1)

            pool.wait_ge(kexp_ok, 4)
            with pool.Fori(0, NP) as p:
                split_keys(0, p)

            pool.wait_ge(d_done, H)
            split_query(0, 0)
            split_query(1, 1)
            pool.wait_ge(c_done, H)
            pool.wait_ge(qabs_ok, H)
            with pool.Fori(0, NP) as p:
                split_query(2 * p + 2, 0)
                sum_chunks(2 * p, 0)
                split_query(2 * p + 3, 1)
                sum_chunks(2 * p + 1, 1)
                split_keys(1, p)
            with pool.Fori(NP, NQT // 2 - 1) as pair:
                split_query(2 * pair + 2, 0)
                sum_chunks(2 * pair, 0)
                split_query(2 * pair + 3, 1)
                sum_chunks(2 * pair + 1, 1)
            sum_chunks(NQT - 2, 0)
            sum_chunks(NQT - 1, 1)

            def mix_qk(t):
                for n, g in enumerate((1, 3)):
                    if n == 0:
                        pool.wait_ge(qkv_ok, t + 1)
                    q = qkv[:, t % 2, 0, :].rearrange("p (h d) -> p h d", d=DK)[:, g * HG:(g + 1) * HG, :]
                    k = qkv[:, t % 2, 1, :].rearrange("p (k d) -> p k d", d=DK)
                    if t:
                        pool.wait_ge(mix_dve, MIX_STEPS * (t - 1) + MIX_FREE[g])
                    nc.gpsimd.tensor_tensor(prod[:, 1 + n], q.unsqueeze(2).to_broadcast([P, HG, H, DK]),
                                            k.unsqueeze(1).to_broadcast([P, HG, H, DK]),
                                            ALU.mult).then_inc(mix_pool, 1)

            def mix_v(t):
                for n, g in enumerate((1, 3)):
                    v = qkv[:, t % 2, 2, :].rearrange("p (k d) -> p d k", d=DK)
                    pool.wait_ge(mix_dve, MIX_STEPS * t + MIX_SUM[g])
                    s = mix[:, g * HG:(g + 1) * HG, :]
                    o = prod[:, 1 + n].rearrange("p h k d -> p h (k d)").rearrange("p h (d k) -> p h d k", k=H)
                    nc.gpsimd.tensor_tensor(o, s.unsqueeze(2).to_broadcast([P, HG, DK, H]),
                                            v.unsqueeze(1).to_broadcast([P, HG, DK, H]),
                                            ALU.mult).then_inc(mix_pool, 1)

            inverse_root(0, 1, 2)
            inverse_root(1, 1, 3)
            mix_qk(0)
            mix_v(0)
            inverse_root(2, 1, 4)
            mix_qk(1)
            mix_v(1)
            inverse_root(3, 1, 5)
            mix_qk(2)
            inverse_root(0, 1, 6)
            inverse_root(1, 1, 7)
            mix_v(2)
            mix_qk(3)
            mix_v(3)
            inverse_root(2, 1, 8)
            inverse_root(3, 1, 9)

        @block.scalar
        def _(act):
            act.wait_ge(x_in, 16)
            for q in range(4):
                cols = slice(q * L // 4, (q + 1) * L // 4)
                act.dma_start(kvr[:, :, cols], kv_v[:, :, cols]).then_inc(kv_in[q], 16)
            for s in (exp_done, hi_done, al_done):
                act.sem_inc(s, SPARE)
            for i in range(2):
                act.sem_inc(hi_in[i], 16 * SPARE)
            act.wait_ge(const_ok, 2)
            for c in range(DC):
                act.wait_ge(xnT_mm, c + 1)
                nc.scalar.copy(xnT[:, c, :], ps_s[:, c, :]).then_inc(xnT_ok, 1)

            def take_qhk(h, i):
                act.wait_ge(a_done, h + 1)
                nc.scalar.copy(qhk[:, i, :], ps_t[:, 0, :]).then_inc(qhk_ok, 1)

            def take_g_d(h, i):
                act.wait_ge(g_done, h + 1)
                nc.scalar.copy(gmat[:, i, :, :].rearrange("p c d -> p (c d)"), ps_t[:, 1, 0:DCQ]).then_inc(g_ok, 1)
                act.wait_ge(d_done, h + 1)
                nc.scalar.copy(wo_abs[:, bass.ds(h * D, D)], ps_o[:, 1, :]).then_inc(d_ok, 1)

            def take_qabs(h):
                act.wait_ge(c_done, h + 1)
                dst = qctx.rearrange("p (b c) -> p b c", b=B)[:, :, bass.ds(h * S, S)]
                nc.scalar.copy(dst, ps_o[:, 0, :].rearrange("p (b s) -> p b s", b=B)).then_inc(qabs_ok, 1)

            take_qhk(0, 0)
            take_qhk(1, 1)
            take_g_d(0, 0)
            with act.Fori(0, (H - 2) // 2) as pair:
                for h, i in ((2 * pair + 1, 1), (2 * pair + 2, 0)):
                    take_qhk(h + 1, 1 - i)
                    take_g_d(h, i)
                    take_qabs(h - 1)
            take_g_d(H - 1, 1)
            take_qabs(H - 2)

            def key_columns(b, g):
                act.wait_ge(ktt_done, 8 * b + g + 1)
                nc.scalar.copy(kt_hi[:, g * HALF:(g + 1) * HALF], ps_t[:, g % 2, :]).then_inc(kth_done, 1)

            act.wait_ge(krope, 4 * NP)
            for g in range(4):
                key_columns(0, g)
            take_qabs(H - 1)
            for g in range(4, 8):
                key_columns(0, g)

            def take_hi(n, half, j):
                act.wait_ge(hi_in[j % 2], 16 * SPARE + 16 * half)
                act.wait_ge(exp_done, SPARE + n + 1)
                nc.scalar.mul(p_hi[:, j % 2, :], prob[:, j % 2, :], PSCALE).then_inc(hi_done, 1)

            def exponents(n, j):
                act.wait_ge(m_done, SPARE + n + 1)
                act.wait_ge(lo_done, SPARE + n - 1)
                i, c = (j // NCH) % 2, j % NCH
                nc.scalar.activation(prob[:, j % 2, :],
                                     ps_s[:, 2 * (j % 2):2 * (j % 2) + 2, :].rearrange("p a c -> p (a c)"),
                                     ACT.Exp, bias=nmax[:, i, c:c + 1], scale=1.0,
                                     accum_out=rsum[:, i, c:c + 1]).then_inc(exp_done, 1)

            def weights_of_chunks(t, i):
                act.wait_ge(nrow_done, SPARE + t + 1)
                nc.scalar.activation(alpha[:, i, :], nmax[:, i, :], ACT.Exp, bias=nrow[:, i, :],
                                     scale=-1.0).then_inc(al_done, 1)

            def head(b, h, last):
                n0 = b * H * NSTEP + h * NSTEP
                for j in range(NSTEP):
                    exponents(n0 + j, j)
                    take_hi(n0 + j, (b * H + h) * (NSTEP // 2) + j // 2, j)
                    if last and b < B - 1 and j in KEY_STEPS:
                        key_columns(b + 1, 2 * (j - KEY_STEPS[0]))
                        key_columns(b + 1, 2 * (j - KEY_STEPS[0]) + 1)
                    if j % NCH == NCH - 1:
                        weights_of_chunks(b * H * TPH + h * TPH + j // NCH, j // NCH)

            for b in range(B):
                with act.Fori(0, H - 1) as h:
                    head(b, h, False)
                head(b, H - 1, True)

            def take_t(n, dst):
                act.wait_ge(tr_done, n + 1)
                nc.scalar.copy(dst, ps_t[:, n % 2, :]).then_inc(tr_ok, 1)

            def ctx_columns(t):
                for g in range(4):
                    if g == 0 and t:
                        act.wait_ge(acc_done, t)
                    take_t(BANKS.index(("ctx", t, g)), ctxT[:, 4 * g:4 * g + 4, :].rearrange("p h s -> p (h s)"))

            def take_qkv(t):
                act.wait_ge(qkv_done, t + 1)
                if t >= 2:
                    act.wait_ge(mix_dve, MIX_STEPS * (t - 1))
                nc.scalar.copy(qkv[:, t % 2, :, :], ps_s[:, 0:3, :]).then_inc(qkv_ok, 1)

            def take_xT(t):
                if t >= 2:
                    act.wait_ge(qkv_done, t - 1)
                take_t(BANKS.index(("x", t)), ynT[:, t % 2, :, :].rearrange("p c s -> p (c s)"))

            def take_mixT(t):
                if t >= 2:
                    act.wait_ge(acc_done, OUTS.index(("mix", t - 2)) + 1)
                take_t(BANKS.index(("mix", t)),
                       mixT[:, 4 * (t % 2):4 * (t % 2) + 4, :].rearrange("p h s -> p (h s)"))

            def take_fT(t):
                if t >= 2:
                    act.wait_ge(f_done, HC)
                n = BANKS.index(("f", t))
                act.wait_ge(tr_done, n + 1)
                nc.scalar.copy(fnT[:, :, t % 2, :],
                               ps_t[:, n % 2, :].rearrange("p (c s) -> p c s", c=DC)).then_inc(tr_ok, 1)

            def shift_gu(j):
                n = 2 * DC * P
                act.wait_ge(wgu_in[j], 16)
                w = wgu[:, j * n:(j + 1) * n]
                nc.scalar.activation(w, w.bitcast(I32), ACT.Copy, bias=-ZERO_POINT, scale=1.0).then_inc(wgu_ok, 1)

            def shift_down():
                act.wait_ge(wdn_in, 16 * 3)
                w = wdn[:, :, :].rearrange("p c n -> p (c n)")
                n = HC * D // 4
                for k in range(4):
                    v = w[:, k * n:(k + 1) * n]
                    nc.scalar.activation(v, v.bitcast(I32), ACT.Copy, bias=-ZERO_POINT, scale=1.0).then_inc(wdn_ok, 1)

            def silu_gate(p, j):
                n = HC * p + j
                act.wait_ge(f_done, n + 1)
                if n >= 2:
                    act.wait_ge(h_ok, n - 1)
                nc.scalar.activation(gact[:, n % 2, :], ps_s[:, n % 4, 0:S], ACT.Silu,
                                     scale=sgu[:, j, 0:1]).then_inc(gact_ok, 1)

            ctx_columns(0)
            ctx_columns(1)
            take_xT(0)
            take_qkv(0)
            shift_down()
            ctx_columns(2)
            take_xT(1)
            take_qkv(1)
            ctx_columns(3)
            take_xT(2)
            take_qkv(2)
            take_mixT(0)
            shift_gu(0)
            take_mixT(1)
            shift_gu(1)
            take_xT(3)
            take_qkv(3)
            take_fT(0)
            take_fT(1)
            for j in range(HC):
                if j + 2 < HC:
                    shift_gu(j + 2)
                silu_gate(0, j)
            take_mixT(2)
            take_mixT(3)
            take_fT(2)
            take_fT(3)
            for j in range(HC):
                silu_gate(1, j)

        @block.vector
        def _(dve):
            dve.wait_ge(x_in, 16)
            for t in range(NT):
                nc.vector.bn_stats(stats[:, t, :], x_in1[:, t, :]).then_inc(st_ln, 1)
            for t in range(NT):
                dve.wait_ge(st_ln, t + 1)
                nc.vector.bn_aggr(mv[:, t, :], stats[:, t, :]).then_inc(st_ln, 1)
            dve.wait_ge(st_ln, 2 * NT)
            nc.vector.tensor_scalar(mv[:, :, 1], mv[:, :, 1], EPS, None, ALU.add).then_inc(var_ok, 1)
            dve.wait_ge(rstd_ok, 1)
            for t in range(NT):
                nc.vector.tensor_scalar(xn[:, t, :], x_in1[:, t, :], mv[:, t, 0:1], rstd[:, t:t + 1],
                                        ALU.subtract, ALU.mult).then_inc(xn_ok, 1)
            for s in (m_done, lo_done, nrow_done, o_used):
                dve.sem_inc(s, SPARE)
            for i in range(2):
                dve.sem_inc(lo_in[i], 16 * SPARE)

            def q_rope(h, i):
                dve.wait_ge(b_done, h + 1)
                q = ps_s[:, 0:QC, :].rearrange("p c (b s) -> p c b s", b=B)
                o = qcos[:, i, :, :].rearrange("p c (b s) -> p c b s", b=B)
                nc.vector.tensor_tensor(o, q, cosq[:, :, :].unsqueeze(2).to_broadcast([P, QC, B, S]), ALU.mult)
                r = qrot[:, i, :, :].rearrange("p c (b s) -> p c b s", b=B)
                for dst, src, p0, p1 in ((0, 1, slice(0, P), slice(0, P)), (1, 0, slice(0, P), slice(0, P)),
                                         (2, 2, slice(0, P // 2), slice(P // 2, P)),
                                         (2, 2, slice(P // 2, P), slice(0, P // 2))):
                    sn = sinq[p1, dst, :]
                    last = nc.vector.tensor_tensor(r[p0, dst, :, :], q[p1, src, :, :],
                                                   sn.unsqueeze(1).to_broadcast([sn.shape[0], B, S]), ALU.mult)
                last.then_inc(rope_mul, 1)
                dve.wait_ge(rope_mul, h + 1)
                nc.vector.tensor_tensor(qcos[:, i, :, :], qcos[:, i, :, :], qrot[:, i, :, :],
                                        ALU.add).then_inc(qrope_ok, 1)

            def largest_key(p):
                dve.wait_ge(krope, 4 * (p + 1))
                nc.vector.tensor_reduce(kmax[:, bass.ds(p, 1)], kvr[:, :, bass.ds(p * PIECE, PIECE)],
                                        mybir.AxisListType.XY, ALU.max,
                                        apply_absolute_value=True).then_inc(kmax_ok, 1)

            dve.wait_ge(tab_in, 32)
            q_rope(0, 0)
            with dve.Fori(0, NP // 2) as pair:
                q_rope(2 * pair + 1, 1)
                largest_key(2 * pair)
                q_rope(2 * pair + 2, 0)
                largest_key(2 * pair + 1)
            dve.wait_ge(kmax_ok, NP)
            nc.vector.tensor_reduce(kmax[:, NP:NP + 1], kmax[:, 0:NP], AX_X, ALU.max).then_inc(kmax_ok, 1)
            q_rope(NP + 1, 1)
            q_rope(NP + 2, 0)
            dve.wait_ge(kmax_all, 1)
            nc.vector.tensor_scalar(kexp[:, 0:1], kmax[:, NP + 1:NP + 2].bitcast(I32), EXP_BITS, None,
                                    ALU.bitwise_and).then_inc(kexp_ok, 1)
            dve.wait_ge(kexp_ok, 1)
            nc.vector.tensor_scalar(kexp[:, 1:2], kexp[:, 0:1], float(15 * EXP_ONE), -1.0, ALU.max,
                                    ALU.mult).then_inc(kexp_ok, 1)
            dve.wait_ge(kexp_ok, 2)
            nc.vector.tensor_scalar(kexp[:, 2:3], kexp[:, 1:2], float(268 * EXP_ONE), None,
                                    ALU.add).then_inc(kexp_ok, 1)
            nc.vector.tensor_scalar(kexp[:, 3:4], kexp[:, 1:2], -1.0, -float(14 * EXP_ONE), ALU.mult,
                                    ALU.add).then_inc(kexp_ok, 1)

            with dve.Fori(NP // 2 + 1, (H - 2) // 2) as pair:
                q_rope(2 * pair + 1, 1)
                q_rope(2 * pair + 2, 0)
            q_rope(H - 1, 1)

            def key_columns(b, g):
                dve.wait_ge(kth_done, 8 * b + g + 1)
                cols = slice(g * HALF, (g + 1) * HALF)
                nc.vector.tensor_tensor(kt_lo[:, cols], ps_t[:, g % 2, :], kt_hi[:, cols].bitcast(F32),
                                        ALU.subtract).then_inc(kt_done, 1)

            def take_lo(n, half, j):
                dve.wait_ge(lo_in[j % 2], 16 * SPARE + 16 * half)
                dve.wait_ge(hi_done, SPARE + n + 1)
                nc.vector.scalar_tensor_tensor(out=p_lo[:, j % 2, :], in0=prob[:, j % 2, :], scalar=PSCALE,
                                               in1=p_hi[:, j % 2, :], op0=ALU.mult,
                                               op1=ALU.subtract).then_inc(lo_done, 1)

            def chunk_maximum(n, j):
                dve.wait_ge(s_done, SPARE + n + 1)
                i, c = (j // NCH) % 2, j % NCH
                nc.vector.tensor_reduce(nmax[:, i, c:c + 1],
                                        ps_s[:, 2 * (j % 2):2 * (j % 2) + 2, :].rearrange("p a c -> p (a c)"),
                                        AX_X, ALU.max, negate=True).then_inc(m_done, 1)

            def row_maximum(t, i):
                dve.wait_ge(m_done, SPARE + NCH * (t + 1))
                nc.vector.tensor_reduce(nrow[:, i, :], nmax[:, i, :], AX_X, ALU.min).then_inc(nrow_done, 1)

            def end_tile(t, i):
                dve.wait_ge(al_done, SPARE + t + 1)
                nc.vector.tensor_tensor_reduce(out=junk[:, i, :], in0=alpha[:, i, :], in1=rsum[:, i, :], scale=PSCALE,
                                               scalar=0.0, op0=ALU.mult, op1=ALU.add,
                                               accum_out=lsum[:, i, :]).then_inc(fin, 1)
                dve.wait_ge(fin, 3 * t + 1)
                nc.vector.reciprocal(lrec[:, i, :], lsum[:, i, :]).then_inc(fin, 1)
                dve.wait_ge(fin, 3 * t + 2)
                nc.vector.tensor_scalar(weigh[:, i, :], alpha[:, i, :], lrec[:, i, :], kunscale,
                                        ALU.mult, ALU.mult).then_inc(fin, 1)
                dve.wait_ge(fin, 3 * t + 3)
                dve.wait_ge(pv_done, SPARE + NCH * (t + 1))
                dve.wait_ge(ctx_done, SPARE + t - 1)
                nc.vector.tensor_tensor(oscl[:, i, :, :], ps_o[:, i, :].rearrange("p (c d) -> p c d", c=NCH),
                                        weigh[:, i, :].unsqueeze(2).to_broadcast([P, NCH, P]),
                                        ALU.mult).then_inc(o_used, 1)

            def head(b, h, first, last):
                n0 = b * H * NSTEP + h * NSTEP
                t0 = b * H * TPH + h * TPH
                for j in range(NSTEP):
                    if j == NCH - 1 and not first:
                        end_tile(t0 - 1, 1)
                    if j == NSTEP - 1:
                        end_tile(t0, 0)
                    if not (last and b == B - 1 and j == NSTEP - 1):
                        chunk_maximum(n0 + j + 1, j + 1)
                    if j % NCH == NCH - 2:
                        row_maximum(t0 + j // NCH, j // NCH)
                    take_lo(n0 + j, (b * H + h) * (NSTEP // 2) + j // 2, j)
                    if last and b < B - 1 and j in KEY_STEPS:
                        key_columns(b + 1, 2 * (j - KEY_STEPS[0]))
                        key_columns(b + 1, 2 * (j - KEY_STEPS[0]) + 1)

            for g in range(8):
                key_columns(0, g)
            chunk_maximum(0, 0)
            for b in range(B):
                head(b, 0, b == 0, False)
                with dve.Fori(1, H - 1) as h:
                    head(b, h, False, False)
                head(b, H - 1, False, True)
            end_tile(NQT - 1, 1)

            def layer_norm(k):
                kind, t = NORMS[k]
                n = OUTS.index(("out", t) if kind == "x" else ("mix", t))
                dve.wait_ge(x_again, 16)
                dve.wait_ge(acc_done, n + 1)
                nc.vector.tensor_tensor(xres[:, t, :], ps_o[:, n % 2, :], xres[:, t, :], ALU.add).then_inc(acc_used, 1)
                dve.wait_ge(acc_used, n + 1)
                nc.vector.bn_stats(stats[:, t, :], xres[:, t, :]).then_inc(st_ln, 1)
                dve.wait_ge(st_ln, 2 * NT + 2 * k + 1)
                nc.vector.bn_aggr(mv[:, t, :], stats[:, t, :]).then_inc(st_ln, 1)
                dve.wait_ge(st_ln, 2 * NT + 2 * k + 2)
                nc.vector.tensor_scalar(mv[:, t, 1:2], mv[:, t, 1:2], EPS, None, ALU.add).then_inc(var_ok, 1)
                dve.wait_ge(rstd_ok, 2 + k)
                if k >= 2:
                    dve.wait_ge(tr_done, max(BANKS.index(NORMS[i]) for i in range(k) if NORMS[i][1] % 2 == t % 2) + 1)
                nc.vector.tensor_scalar(yn[:, t % 2, :], xres[:, t, :], mv[:, t, 0:1], rstd[:, t:t + 1],
                                        ALU.subtract, ALU.mult).then_inc(yn_ok, 1)

            def mix_step(t, m):
                what, g = MIX_ORDER[m]
                heads = slice(g * HG, (g + 1) * HG)
                done = MIX_STEPS * t + m
                slot = 0 if g % 2 == 0 else 1 + g // 2
                by_k = prod[:, slot]
                by_d = by_k.rearrange("p h k d -> p h (k d)").rearrange("p h (d k) -> p h d k", k=H)
                if what == "mul":
                    if m == 0:
                        dve.wait_ge(qkv_ok, t + 1)
                    if done:
                        dve.wait_ge(mix_dve, done)
                    q = qkv[:, t % 2, 0, :].rearrange("p (h d) -> p h d", d=DK)[:, heads, :]
                    k = qkv[:, t % 2, 1, :].rearrange("p (k d) -> p k d", d=DK)
                    last = nc.vector.tensor_tensor(by_k, q.unsqueeze(2).to_broadcast([P, HG, H, DK]),
                                                   k.unsqueeze(1).to_broadcast([P, HG, H, DK]), ALU.mult)
                elif what == "sum":
                    if g % 2:
                        dve.wait_ge(mix_pool, 4 * t + 1 + g // 2)
                    dve.wait_ge(mix_dve, done)
                    last = nc.vector.tensor_reduce(mix[:, heads, :], by_k, AX_X, ALU.add)
                elif what == "mulv":
                    dve.wait_ge(mix_dve, done)
                    v = qkv[:, t % 2, 2, :].rearrange("p (k d) -> p d k", d=DK)
                    last = nc.vector.tensor_tensor(by_d, mix[:, heads, :].unsqueeze(2).to_broadcast([P, HG, DK, H]),
                                                   v.unsqueeze(1).to_broadcast([P, HG, DK, H]), ALU.mult)
                else:
                    if g % 2:
                        dve.wait_ge(mix_pool, 4 * t + 3 + g // 2)
                    dve.wait_ge(mix_dve, done)
                    if t >= 2:
                        dve.wait_ge(tr_done, BANKS.index(("mix", t - 2)) + 1)
                    o = mixo[:, t % 2, :].rearrange("p (h d) -> p h d", d=DK)[:, heads, :]
                    last = nc.vector.tensor_reduce(o, by_d, AX_X, ALU.add)
                last.then_inc(mix_dve, 1)

            def gate_up(p, j):
                n = HC * p + j
                dve.wait_ge(gact_ok, n + 1)
                if p:
                    dve.wait_ge(acc_done, OUTS.index(("down", TPH - 1)) + 1)
                nc.vector.scalar_tensor_tensor(out=hT[:, j, :], in0=ps_s[:, n % 4, S:2 * S], scalar=sgu[:, j, 1:2],
                                               in1=gact[:, n % 2, :], op0=ALU.mult, op1=ALU.mult).then_inc(h_ok, 1)

            def finish(t):
                n = OUTS.index(("down", t))
                dve.wait_ge(acc_done, n + 1)
                if t:
                    dve.wait_ge(y_ok, t)
                nc.vector.tensor_tensor(dsc[:, :], ps_o[:, n % 2, :], sdn[:, :], ALU.mult).then_inc(acc_used, 1)
                dve.wait_ge(acc_used, n + 1)
                nc.vector.tensor_tensor(xres[:, t, :], dsc[:, :], xres[:, t, :], ALU.add).then_inc(y_ok, 1)

            h_next = 0
            layer_norm(0)
            layer_norm(1)
            for m in range(MIX_STEPS):
                mix_step(0, m)
            layer_norm(2)
            for m in range(MIX_STEPS):
                mix_step(1, m)
            layer_norm(3)
            for m in range(MIX_STEPS // 2):
                mix_step(2, m)
            layer_norm(4)
            layer_norm(5)
            dve.wait_ge(wdn_in, 16 * 3)
            for m in range(MIX_STEPS // 2, 2 * MIX_STEPS):
                mix_step(2 + m // MIX_STEPS, m % MIX_STEPS)
                if m % 3 != 1 and h_next < HC:
                    gate_up(0, h_next)
                    h_next += 1
            for j in range(h_next, HC):
                gate_up(0, j)
            finish(0)
            finish(1)
            layer_norm(6)
            layer_norm(7)
            for j in range(HC):
                gate_up(1, j)
            finish(2)
            finish(3)

        @block.tensor
        def _(pe):
            for s in (s_done, pv_done):
                pe.sem_inc(s, SPARE)
            pe.wait_ge(const_ok, 3)
            pe.wait_ge(xn_ok, NT)
            for c in range(DC):
                for t in range(NT):
                    last = nc.tensor.transpose(ps_s[:, c, t * P:(t + 1) * P], xn[:, t, c * P:(c + 1) * P], ident[:, :])
                last.then_inc(xnT_mm, 1)
            pe.wait_ge(xnT_ok, DC)

            def q_head(h, i, k, first=False):
                pe.wait_ge(wq_in[i], 16 * k)
                if not first:
                    pe.wait_ge(qhk_ok, h)
                for c in range(DC):
                    last = nc.tensor.matmul(ps_t[:, 0, :], wq_s[:, i, c, :], xnT[:, c, :],
                                            start=(c == 0), stop=(c == DC - 1))
                last.then_inc(a_done, 1)

            def q_wide(h, i, k, first=False):
                pe.wait_ge(wkcq_in[i], 16 * k)
                pe.wait_ge(qhk_ok, h + 1)
                if not first:
                    pe.wait_ge(rope_mul, h)
                for c in range(QC):
                    last = nc.tensor.matmul(ps_s[:, c, :], wkcq_s[:, i, c * P:(c + 1) * P], qhk[:, i, :],
                                            start=True, stop=True)
                last.then_inc(b_done, 1)

            def fused_weights(h, i, k, first=False):
                pe.wait_ge(wrest_in[i], 64 * k)
                if not first:
                    pe.wait_ge(g_ok, h)
                for c in range(QC):
                    last = nc.tensor.matmul(ps_t[:, 1, c * P:(c + 1) * P], wqr_s[:, i, c * P:(c + 1) * P],
                                            wkr_s[:, i, :], start=True, stop=True)
                last.then_inc(g_done, 1)
                if not first:
                    pe.wait_ge(d_ok, h)
                nc.tensor.matmul(ps_o[:, 1, :], wkckv_s[:, i, :], wot_s[:, i, :],
                                 start=True, stop=True).then_inc(d_done, 1)

            def q_absorbed(h, i, first=False):
                pe.wait_ge(qrope_ok, h + 1)
                pe.wait_ge(g_ok, h + 1)
                if not first:
                    pe.wait_ge(qabs_ok, h)
                for c in range(QC):
                    last = nc.tensor.matmul(ps_o[:, 0, :], gmat[:, i, c, :], qcos[:, i, c, :],
                                            start=(c == 0), stop=(c == QC - 1))
                last.then_inc(c_done, 1)

            q_head(0, 0, 1, True)
            q_wide(0, 0, 1, True)
            q_head(1, 1, 1)
            fused_weights(0, 0, 1, True)
            q_wide(1, 1, 1)
            q_head(2, 0, 2)
            fused_weights(1, 1, 1)
            q_absorbed(0, 0, True)
            with pe.Fori(0, (H - 4) // 2) as pair:
                for h, i, k in ((2 * pair + 2, 0, pair + 2), (2 * pair + 3, 1, pair + 2)):
                    q_wide(h, i, k)
                    q_head(h + 1, 1 - i, k + i)
                    fused_weights(h, i, k)
                    q_absorbed(h - 1, 1 - i)
            q_wide(H - 2, 0, H // 2)
            q_head(H - 1, 1, H // 2)
            fused_weights(H - 2, 0, H // 2)
            q_absorbed(H - 3, 1)
            q_wide(H - 1, 1, H // 2)
            fused_weights(H - 1, 1, H // 2)
            q_absorbed(H - 2, 0)

            def key_columns(b, g):
                for k in range(4):
                    blk = 4 * g + k
                    last = nc.tensor.transpose(ps_t[:, g % 2, k * P:(k + 1) * P],
                                               kvr[:, b, blk * P:(blk + 1) * P], ident[:, :])
                last.then_inc(ktt_done, 1)

            pe.wait_ge(krope, 4 * NP)
            pe.wait_ge(qhk_ok, H)
            pe.wait_ge(g_ok, H)
            for g in range(4):
                if g >= 2:
                    pe.wait_ge(kt_done, g - 1)
                key_columns(0, g)
            q_absorbed(H - 1, 1)
            for g in range(4, 8):
                pe.wait_ge(kt_done, g - 1)
                key_columns(0, g)

            def scores(n, j):
                pe.wait_ge(exp_done, SPARE + n - 1)
                i, c = (j // NCH) % 2, j % NCH
                for a in range(2):
                    o = ps_s[:, 2 * (j % 2) + a, :]
                    cols = slice(c * CHUNK + a * HALF, c * CHUNK + (a + 1) * HALF)
                    nc.tensor.matmul(o, q_hi[:, i, :], kt_hi[:, cols], start=True, stop=False)
                    nc.tensor.matmul(o, q_hi[:, i, :], kt_lo[:, cols], start=False, stop=False)
                    last = nc.tensor.matmul(o, q_lo[:, i, :], kt_hi[:, cols], start=False, stop=True)
                last.then_inc(s_done, 1)

            def weighed_keys(b, half, t, j):
                i, c = (j // NCH) % 2, j % NCH
                if c == 0:
                    pe.wait_ge(o_used, SPARE + t - 1)
                o = ps_o[:, i, c * P:(c + 1) * P]
                pe.wait_ge(hi_in[j % 2], 16 * SPARE + 16 * (half + 1))
                for k in range(CHUNK // P):
                    keys = slice((c * (CHUNK // P) + k) * P, (c * (CHUNK // P) + k + 1) * P)
                    nc.tensor.matmul(o, pt_hi[:, j % 4, k, :], kn_hi[b][:, keys], start=(k == 0), stop=False)
                    nc.tensor.matmul(o, pt_hi[:, j % 4, k, :], kn_lo[b][:, keys], start=False, stop=False)
                pe.wait_ge(lo_in[j % 2], 16 * SPARE + 16 * (half + 1))
                for k in range(CHUNK // P):
                    keys = slice((c * (CHUNK // P) + k) * P, (c * (CHUNK // P) + k + 1) * P)
                    last = nc.tensor.matmul(o, pt_lo[:, j % 4, k, :], kn_hi[b][:, keys], start=False,
                                            stop=(k == CHUNK // P - 1))
                last.then_inc(pv_done, 1)

            def head(b, h, first, last):
                n0 = b * H * NSTEP + h * NSTEP
                t0 = b * H * TPH + h * TPH
                for j in range(NSTEP):
                    if not (last and b == B - 1 and j >= NSTEP - AHEAD):
                        if (j + AHEAD) % NCH == 0:
                            pe.wait_ge(q_ready, SPARE + t0 + (j + AHEAD) // NCH + 1)
                        if last and j >= NSTEP - AHEAD:
                            pe.wait_ge(kt_done, 8 * (b + 1) + 2 * (j - NSTEP + AHEAD + 1))
                        scores(n0 + j + AHEAD, j + AHEAD)
                    if last and b < B - 1 and j < NCH:
                        for g in (2 * j, 2 * j + 1):
                            pe.wait_ge(kt_done, 8 * (b + 1) + g - 1)
                            key_columns(b + 1, g)
                    if first and j < NCH:
                        pe.wait_ge(kn_done, 2 * (j + 1) if b == 0 else KN_DONE)
                    weighed_keys(b, (b * H + h) * (NSTEP // 2) + j // 2, t0 + j // NCH, j)

            pe.wait_ge(rope_mul, H)
            pe.wait_ge(q_ready, SPARE + 1)
            for n in range(AHEAD):
                pe.wait_ge(kt_done, 2 * (n + 1))
                scores(n, n)
            pe.wait_ge(qabs_ok, H)
            pe.wait_ge(d_ok, H)
            for b in range(B):
                head(b, 0, True, False)
                with pe.Fori(1, H - 1) as h:
                    head(b, h, False, False)
                head(b, H - 1, False, True)

            def turn(bank, src, ready, count):
                n = BANKS.index(bank)
                pe.wait_ge(ready, count)
                if n >= 2:
                    pe.wait_ge(tr_ok, n - 1)
                for k in range(4):
                    last = nc.tensor.transpose(ps_t[:, n % 2, k * P:(k + 1) * P], src(k), ident[:, :])
                last.then_inc(tr_done, 1)

            def ready_out(n):
                if n >= 2:
                    pe.wait_ge(acc_used, n - 1)
                else:
                    pe.wait_ge(o_used, SPARE + NQT - 1 + n)
                return ps_o[:, n % 2, :]

            def context_out(t):
                for g in range(4):
                    turn(("ctx", t, g), lambda k: qctx[:, ctx_tile(t, 4 * g + k):ctx_tile(t, 4 * g + k) + P],
                         ctx_done, SPARE + NQT // B * (t // TPH + 1))
                pe.wait_ge(tr_ok, BANKS.index(("ctx", t, 3)) + 1)
                o = ready_out(OUTS.index(("out", t)))
                for h in range(H):
                    last = nc.tensor.matmul(o, ctxT[:, h, :], wo_abs[:, h * D:(h + 1) * D],
                                            start=(h == 0), stop=(h == H - 1))
                last.then_inc(acc_done, 1)

            def turn_norm(k):
                kind, t = NORMS[k]
                turn((kind, t), lambda c: yn[:, t % 2, c * P:(c + 1) * P], yn_ok, k + 1)

            def mix_in(t):
                pe.wait_ge(tr_ok, BANKS.index(("x", t)) + 1)
                pe.wait_ge(wmix_in, 16 * H)
                if t:
                    pe.wait_ge(qkv_ok, t)
                for m in range(3):
                    for c in range(DC):
                        last = nc.tensor.matmul(ps_s[:, m, :], ynT[:, t % 2, c, :],
                                                wmix[:, (m * DC + c) * D:(m * DC + c + 1) * D],
                                                start=(c == 0), stop=(c == DC - 1))
                last.then_inc(qkv_done, 1)

            def mix_out(t):
                turn(("mix", t), lambda c: mixo[:, t % 2, c * P:(c + 1) * P], mix_dve, MIX_STEPS * (t + 1))
                pe.wait_ge(tr_ok, BANKS.index(("mix", t)) + 1)
                o = ready_out(OUTS.index(("mix", t)))
                for c in range(DC):
                    last = nc.tensor.matmul(o, mixT[:, 4 * (t % 2) + c, :],
                                            wmix[:, (3 * DC + c) * D:(3 * DC + c + 1) * D],
                                            start=(c == 0), stop=(c == DC - 1))
                last.then_inc(acc_done, 1)

            def gate_up(p):
                pe.wait_ge(tr_ok, BANKS.index(("f", 2 * p + 1)) + 1)
                for j in range(HC):
                    n = HC * p + j
                    pe.wait_ge(wgu_ok, j + 1)
                    if n >= 4:
                        pe.wait_ge(h_ok, n - 3)
                    else:
                        pe.wait_ge(qkv_ok, NT)
                    for m in range(2):
                        for c in range(DC):
                            w = wgu[:, ((2 * j + m) * DC + c) * P:((2 * j + m) * DC + c + 1) * P]
                            last = nc.tensor.matmul(ps_s[:, n % 4, m * S:(m + 1) * S], w,
                                                    fnT[:, c, :, :].rearrange("p u s -> p (u s)"),
                                                    start=(c == 0), stop=(c == DC - 1))
                    last.then_inc(f_done, 1)

            def down(t):
                pe.wait_ge(h_ok, HC * (t // TPH + 1))
                pe.wait_ge(wdn_ok, 4)
                o = ready_out(OUTS.index(("down", t)))
                for j in range(HC):
                    last = nc.tensor.matmul(o, hT[:, j, (t % TPH) * P:(t % TPH + 1) * P], wdn[:, j, :],
                                            start=(j == 0), stop=(j == HC - 1))
                last.then_inc(acc_done, 1)

            context_out(0)
            context_out(1)
            turn_norm(0)
            mix_in(0)
            context_out(2)
            turn_norm(1)
            mix_in(1)
            context_out(3)
            turn_norm(2)
            mix_in(2)
            mix_out(0)
            mix_out(1)
            turn_norm(3)
            mix_in(3)
            turn_norm(4)
            turn_norm(5)
            gate_up(0)
            down(0)
            down(1)
            mix_out(2)
            mix_out(3)
            turn_norm(6)
            turn_norm(7)
            gate_up(1)
            down(2)
            down(3)


MIX_ORDER = [("mul", 0), ("sum", 0), ("mul", 2), ("sum", 2), ("sum", 1), ("sum", 3),
             ("mulv", 0), ("sumv", 0), ("mulv", 2), ("sumv", 2), ("sumv", 1), ("sumv", 3)]
MIX_STEPS = len(MIX_ORDER)
MIX_SUM = {g: MIX_ORDER.index(("sum", g)) + 1 for g in range(4)}
MIX_FREE = {g: MIX_ORDER.index(("sumv", g)) + 1 for g in range(4)}
KEY_STEPS = range(3, 7)

BANKS = ([("ctx", 0, g) for g in range(4)] + [("ctx", 1, g) for g in range(4)] + [("x", 0)]
         + [("ctx", 2, g) for g in range(4)] + [("x", 1)] + [("ctx", 3, g) for g in range(4)]
         + [("x", 2), ("mix", 0), ("mix", 1), ("x", 3), ("f", 0), ("f", 1),
            ("mix", 2), ("mix", 3), ("f", 2), ("f", 3)])
OUTS = [("out", 0), ("out", 1), ("out", 2), ("out", 3), ("mix", 0), ("mix", 1), ("down", 0), ("down", 1),
        ("mix", 2), ("mix", 3), ("down", 2), ("down", 3)]
NORMS = [("x", 0), ("x", 1), ("x", 2), ("x", 3), ("f", 0), ("f", 1), ("f", 2), ("f", 3)]


def ctx_tile(t, h):
    return ((t // TPH * H + h) * TPH + t % TPH) * P


def rope_tables(length, dim):
    inv = (np.float32(1.0) / np.power(np.float32(10000.0), np.arange(0, dim, 2, dtype=np.float32)
                                      / np.float32(dim)).astype(np.float32)).astype(np.float32)
    f = (np.arange(length, dtype=np.float32)[:, None] * inv[None, :]).astype(np.float32)
    sin = np.repeat(np.sin(f), 2, axis=-1).astype(np.float32)
    cos = np.repeat(np.cos(f), 2, axis=-1).astype(np.float32)
    sin[:, :dim // 2] *= -1
    return sin, cos


def kernel(x, ctx_512, L0_xattn_Wq, L0_xattn_w_kc_q, L0_xattn_w_kc_kv, L0_xattn_W_qr, L0_xattn_W_kr,
           L0_xattn_Wo, L0_attn_Wq, L0_attn_Wk, L0_attn_Wv, L0_attn_Wo, L0_ffn_wq_gate, L0_ffn_s_gate,
           L0_ffn_wq_up, L0_ffn_s_up, L0_ffn_wq_down, L0_ffn_s_down):
    import concourse.bacc as bacc
    from concourse.bass_utils import run_bass_kernel_spmd

    half = DCQ // 2
    perm = np.concatenate([np.arange(0, P), np.arange(half, half + P), np.arange(P, half),
                           np.arange(half + P, DCQ)])
    sin, cos = rope_tables(S, DCQ)
    cos_q = cos.T[perm].reshape(QC, P, S).transpose(1, 0, 2).reshape(P, QC * S)
    sq = sin.T[perm].reshape(QC, P, S)
    sq = np.stack([sq[0], sq[1], np.concatenate([sq[2, P // 2:], sq[2, :P // 2]])])
    sin_q = sq.transpose(1, 0, 2).reshape(P, QC * S)
    sin, cos = rope_tables(L, P)
    gate = np.asarray(L0_ffn_wq_gate).T.reshape(DC, P, HC, P)
    up = np.asarray(L0_ffn_wq_up).T.reshape(DC, P, HC, P)
    ins = {
        "x": x,
        "ctx_kv": ctx_512,
        "wq_t": np.asarray(L0_xattn_Wq).reshape(H, P, DC, P).transpose(0, 3, 2, 1).reshape(H, P, DC * P),
        "w_kcq": np.asarray(L0_xattn_w_kc_q)[:, :, perm],
        "w_qr_t": np.asarray(L0_xattn_W_qr)[:, perm, :].transpose(0, 2, 1),
        "w_kr_t": np.asarray(L0_xattn_W_kr).transpose(0, 2, 1),
        "w_kckv": L0_xattn_w_kc_kv,
        "wo_t": np.asarray(L0_xattn_Wo).T.reshape(H, P, D),
        "cos_q": cos_q,
        "sin_q": sin_q,
        "cos_k": cos.reshape(P, L),
        "sin_k": sin.reshape(P, L),
        "w_mix": np.concatenate([np.asarray(w).reshape(DC, P, D).transpose(1, 0, 2).reshape(P, DC * D)
                                 for w in (L0_attn_Wq, L0_attn_Wk, L0_attn_Wv, L0_attn_Wo)], axis=1),
        "w_gu": np.stack([gate, up]).transpose(2, 3, 0, 1, 4).reshape(P, HC * 2 * DC * P),
        "w_dn": np.asarray(L0_ffn_wq_down).T.reshape(HC, P, D).transpose(1, 0, 2).reshape(P, HC * D),
        "s_gu": np.stack([np.asarray(L0_ffn_s_gate), np.asarray(L0_ffn_s_up)], axis=-1)
                  .reshape(HC, P, 2).transpose(1, 0, 2).reshape(P, HC * 2),
        "s_dn": L0_ffn_s_down,
    }
    nc = bacc.Bacc("TRN2", target_bir_lowering=False, num_devices=1)
    arrays, aps = {}, {}
    for name, a in ins.items():
        a = np.ascontiguousarray(a)
        arrays[f"{name}_dram"] = a
        aps[name] = nc.dram_tensor(f"{name}_dram", list(a.shape), mybir.dt.from_np(a.dtype), kind="ExternalInput").ap()
    out = nc.dram_tensor("out_dram", [B, S, D], F32, kind="ExternalOutput").ap()
    build(nc, out=out, **aps)
    r = run_bass_kernel_spmd(nc, [arrays], core_ids=[0])
    return r.results[0]["out_dram"]
```

```python
from contextlib import ExitStack

import numpy as np

import concourse.bass as bass
from concourse import mybir

F32 = mybir.dt.float32
F32R = mybir.dt.float32r
F16 = mybir.dt.float16
I32 = mybir.dt.int32
ALU = mybir.AluOpType
ACT = mybir.ActivationFunctionType
AX_X = mybir.AxisListType.X

P = 128
B, S, D = 2, 256, 512
NT = B * S // P
DC = D // P
H = 16
L = 4096
DCQ, R = 384, 64
QC = DCQ // P
CHUNK = 1024
NCH = L // CHUNK
HALF = 512
LB = L // P
TPH = S // P
NSTEP = NCH * TPH
PIECE = 512
NP = L // PIECE
HID = 1408
HC = HID // P
DK = D // H
HG = 4
EPS = 1e-5
ZERO_POINT = 128.0
PSCALE = 2.0 ** 14
EXP_BITS = 0x7F800000
EXP_ONE = 1 << 23
AHEAD = 4
SPARE = 8


def build(nc, x, ctx_kv, wq_t, w_kcq, w_qr_t, w_kr_t, w_kckv, wo_t, cos_q, sin_q, cos_k, sin_k,
          w_mix, w_gu, w_dn, s_gu, s_dn, out):
    with ExitStack() as stack:
        def sem(name):
            return stack.enter_context(nc.semaphore(name))

        def sb(st, name, shape, dt=F32):
            return st.enter_context(nc.sbuf_tensor(name, shape, dt))

        ps_s = stack.enter_context(nc.psum_tensor("ps_s", [P, 4, HALF], F32))
        ps_t = stack.enter_context(nc.psum_tensor("ps_t", [P, 2, HALF], F32))
        ps_o = stack.enter_context(nc.psum_tensor("ps_o", [P, 2, HALF], F32))

        ident = sb(stack, "ident", [P, P])
        with ExitStack() as st:
            wgu_raw = sb(st, "wgu_raw", [P, HC * 2 * DC * P], I32)
        with ExitStack() as st:
            wgu = sb(st, "wgu", [P, HC * 2 * DC * P], F32R)
        arena = sb(stack, "arena", [P, 2 * H * B * S])
        qctx = arena[:, 0:H * B * S]
        wo_abs = arena[:, H * B * S:2 * H * B * S]
        with ExitStack() as st:
            hT = sb(st, "hT", [P, 2, HC * S], F32R)
        kvr = sb(stack, "kvr", [P, B, L])
        stats = sb(stack, "stats", [P, NT, 6])
        mv = sb(stack, "mv", [P, NT, 2])
        rstd = sb(stack, "rstd", [P, NT])
        mhalf = sb(stack, "mhalf", [P, NT])
        kmax = sb(stack, "kmax", [P, NP + 2])
        kexp = sb(stack, "kexp", [P, 4], I32)
        kscale = kexp[:, 2:3].bitcast(F32)
        kunscale = kexp[:, 3:4].bitcast(F32)
        yn = sb(stack, "yn", [P, 2, D])
        with ExitStack() as keys:
            kn0_hi = sb(keys, "kn0_hi", [P, L], F16)
            kn0_lo = sb(keys, "kn0_lo", [P, L], F16)
            kn_raw = sb(keys, "kn_raw", [P, PIECE])
            with ExitStack() as st:
                with ExitStack() as once:
                    x_in1 = sb(once, "x_in1", [P, NT, D])
                xnT_hi = sb(st, "xnT_hi", [P, DC, B * S], F32R)
                cs_k = sb(st, "cs_k", [P, 2, 2, PIECE])
                krot = sb(st, "krot", [P, B, PIECE])
                xnT_lo = sb(st, "xnT_lo", [P, DC, B * S], F32R)
                with ExitStack() as once:
                    wq_s = sb(once, "wq_s", [P, 2, DC, P])
                wq_lo = sb(st, "wq_lo", [P, 2, DC, P], F32R)
                wq_hi = sb(st, "wq_hi", [P, 2, DC, P], F32R)
                wkcq_s = sb(st, "wkcq_s", [P, 2, DCQ])
                wqr_s = sb(st, "wqr_s", [R, 2, DCQ])
                wkr_s = sb(st, "wkr_s", [R, 2, P])
                wkckv_s = sb(st, "wkckv_s", [P, 2, P])
                wot_s = sb(st, "wot_s", [P, 2, D])
                cosq = sb(st, "cosq", [P, QC, S])
                sinq = sb(st, "sinq", [P, QC, S])
                qhk = sb(st, "qhk", [P, 2, B * S])
                gmat = sb(st, "gmat", [P, 2, QC, P])
                qcos = sb(st, "qcos", [P, 2, QC, B * S])
                qrot = sb(st, "qrot", [P, 2, QC, B * S])
                xn = qrot[:, :, :, :].rearrange("p i c s -> p (i c s)")[:, 0:NT * D]\
                    .rearrange("p (t d) -> p t d", d=D)
            with ExitStack() as st:
                kt_hi = sb(st, "kt_hi", [P, L], F32R)
                kt_lo = sb(st, "kt_lo", [P, L], F32R)
                q_hi = sb(st, "q_hi", [P, 2, P], F32R)
                q_lo = sb(st, "q_lo", [P, 2, P], F32R)
                prob = sb(st, "prob", [P, 2, CHUNK])
                p_hi = sb(st, "p_hi", [P, 2, CHUNK], F16)
                p_lo = sb(st, "p_lo", [P, 2, CHUNK], F16)
                pt_hi = sb(st, "pt_hi", [P, 4, CHUNK // P, P], F16)
                pt_lo = sb(st, "pt_lo", [P, 4, CHUNK // P, P], F16)
                nmax = sb(st, "nmax", [P, 2, NCH])
                nrow = sb(st, "nrow", [P, 2, 1])
                rsum = sb(st, "rsum", [P, 2, NCH])
                alpha = sb(st, "alpha", [P, 2, NCH])
                weigh = sb(st, "weigh", [P, 2, NCH])
                junk = sb(st, "junk", [P, 2, NCH])
                lsum = sb(st, "lsum", [P, 2, 1])
                lrec = sb(st, "lrec", [P, 2, 1])
                oscl = sb(st, "oscl", [P, 2, NCH, P])
                osum = sb(st, "osum", [P, 2, P])
                kn1_hi = sb(st, "kn1_hi", [P, L], F16)
                kn1_lo = sb(st, "kn1_lo", [P, L], F16)
        xres = sb(stack, "xres", [P, NT, D])
        ctxT = sb(stack, "ctxT", [P, H, P])
        with ExitStack() as st:
            wdn_raw = sb(st, "wdn_raw", [P, HC, D], I32)
        with ExitStack() as st:
            wdn = sb(st, "wdn", [P, HC, D], F32R)
            ynT = sb(st, "ynT", [P, 2, DC, P])
            fnT_hi = sb(st, "fnT_hi", [P, DC, TPH, P], F32R)
            fnT_lo = sb(st, "fnT_lo", [P, DC, TPH, P], F32R)
            qkv = sb(st, "qkv", [P, 2, 3, D])
            prod = sb(st, "prod", [P, 3, HG, H, DK])
            mix = sb(st, "mix", [P, H, H])
            mixo = sb(st, "mixo", [P, 2, D])
            gact = sb(st, "gact", [P, 2, S])
            hid = sb(st, "hid", [P, 2, S])
            sgu = sb(st, "sgu", [P, HC, 2])
            sdn = sb(st, "sdn", [P, D])
            dsc = sb(st, "dsc", [P, D])
            mixT = sb(st, "mixT", [P, 2 * DC, P])
        kn_hi, kn_lo = (kn0_hi, kn1_hi), (kn0_lo, kn1_lo)
        wmix = kvr[:, :, :].rearrange("p b c -> p (b c)")
        hT_hi, hT_lo = hT[:, 0, :], hT[:, 1, :]

        x_in = sem("x_in")
        x_again = sem("x_again")
        tab_in = sem("tab_in")
        kv_in = [sem(f"kv_in{i}") for i in range(4)]
        cs_in = [sem(f"cs_in{i}") for i in range(2)]
        wq_in = [sem(f"wq_in{i}") for i in range(2)]
        wkcq_in = [sem(f"wkcq_in{i}") for i in range(2)]
        wrest_in = [sem(f"wrest_in{i}") for i in range(2)]
        const_ok = sem("const_ok")
        st_ln = sem("st_ln")
        var_ok = sem("var_ok")
        rstd_ok = sem("rstd_ok")
        xn_ok = sem("xn_ok")
        xnT_mm = sem("xnT_mm")
        xnTh_ok = sem("xnTh_ok")
        xnT_ok = sem("xnT_ok")
        wqh_ok = sem("wqh_ok")
        wq_ok = sem("wq_ok")
        a_done = sem("a_done")
        b_done = sem("b_done")
        g_done = sem("g_done")
        d_done = sem("d_done")
        c_done = sem("c_done")
        qhk_ok = sem("qhk_ok")
        g_ok = sem("g_ok")
        d_ok = sem("d_ok")
        qabs_ok = sem("qabs_ok")
        rope_mul = sem("rope_mul")
        qrope_ok = sem("qrope_ok")
        kmax_ok = sem("kmax_ok")
        kmax_all = sem("kmax_all")
        kexp_ok = sem("kexp_ok")
        krope = sem("krope")
        ktt_done = sem("ktt_done")
        kth_done = sem("kth_done")
        kt_done = sem("kt_done")
        knh_done = sem("knh_done")
        kn_done = sem("kn_done")
        s_done = sem("s_done")
        m_done = sem("m_done")
        exp_done = sem("exp_done")
        turn_go = sem("turn_go")
        hi_in = [sem(f"hi_in{i}") for i in range(2)]
        lo_in = [sem(f"lo_in{i}") for i in range(2)]
        hi_done = sem("hi_done")
        lo_done = sem("lo_done")
        pv_done = sem("pv_done")
        nrow_done = sem("nrow_done")
        al_done = sem("al_done")
        fin = sem("fin")
        o_used = sem("o_used")
        ctx_half = sem("ctx_half")
        ctx_done = sem("ctx_done")
        qh_done = sem("qh_done")
        q_ready = sem("q_ready")
        wmix_in = sem("wmix_in")
        wdn_in = sem("wdn_in")
        wgu_in = [sem(f"wgu_in{j}") for j in range(HC)]
        tr_done = sem("tr_done")
        tr_ok = sem("tr_ok")
        acc_done = sem("acc_done")
        acc_used = sem("acc_used")
        qkv_done = sem("qkv_done")
        qkv_ok = sem("qkv_ok")
        yn_ok = sem("yn_ok")
        mix_dve = sem("mix_dve")
        mix_pool = sem("mix_pool")
        wdn_ok = sem("wdn_ok")
        wgu_ok = sem("wgu_ok")
        f_done = sem("f_done")
        gact_ok = sem("gact_ok")
        fh_ok = sem("fh_ok")
        hid_ok = sem("hid_ok")
        hh_ok = sem("hh_ok")
        h_ok = sem("h_ok")
        y_ok = sem("y_ok")
        y_out = sem("y_out")

        block = stack.enter_context(nc.Block())
        x_v = x.rearrange("b (u p) d -> p (b u) d", p=P)
        out_v = out.rearrange("b (u p) d -> p (b u) d", p=P)
        kv_v = ctx_kv.rearrange("b (p c) d -> p b (c d)", c=LB)
        NQT = B * H * TPH
        KN_DONE = B * NP
        NCHUNK = NQT * NCH
        T0 = 4 * H

        @block.sync
        def _(sp):
            def load_wq(h, i):
                sp.dma_start(wq_s[:, i, :, :].rearrange("p c k -> p (c k)"),
                             wq_t[bass.ds(h, 1), :, :].rearrange("h p n -> p (h n)")).then_inc(wq_in[i], 16)

            def load_wkcq(h, i):
                sp.dma_start(wkcq_s[:, i, :],
                             w_kcq[bass.ds(h, 1), :, :].rearrange("h p n -> p (h n)")).then_inc(wkcq_in[i], 16)

            def load_rest(h, i):
                for dst, src in ((wqr_s, w_qr_t), (wkr_s, w_kr_t), (wkckv_s, w_kckv), (wot_s, wo_t)):
                    sp.dma_start(dst[:, i, :],
                                 src[bass.ds(h, 1), :, :].rearrange("h p n -> p (h n)")).then_inc(wrest_in[i], 16)

            def load_turn(p, i):
                for m, src in ((0, cos_k), (1, sin_k)):
                    sp.dma_start(cs_k[:, i, m, :], src[:, bass.ds(p * PIECE, PIECE)]).then_inc(cs_in[i], 16)

            sp.dma_start(x_in1[:, :, :], x_v).then_inc(x_in, 16)
            load_wq(0, 0)
            load_wkcq(0, 0)
            sp.dma_start(cosq[:, :, :].rearrange("p c s -> p (c s)"), cos_q).then_inc(tab_in, 16)
            sp.dma_start(sinq[:, :, :].rearrange("p c s -> p (c s)"), sin_q).then_inc(tab_in, 16)
            load_rest(0, 0)
            load_turn(0, 0)
            load_wq(1, 1)
            load_wkcq(1, 1)
            load_rest(1, 1)
            load_turn(1, 1)

            def refill(h, i):
                sp.wait_ge(a_done, h + 1)
                load_wq(h + 2, i)
                sp.wait_ge(b_done, h + 1)
                load_wkcq(h + 2, i)
                sp.wait_ge(d_done, h + 1)
                load_rest(h + 2, i)

            with sp.Fori(0, (NP - 2) // 2) as pair:
                for h, i in ((2 * pair, 0), (2 * pair + 1, 1)):
                    refill(h, i)
                    sp.wait_ge(krope, 4 * (h + 1))
                    load_turn(h + 2, i)
            with sp.Fori((NP - 2) // 2, (H - 2) // 2) as pair:
                refill(2 * pair, 0)
                refill(2 * pair + 1, 1)

            def turn_exponents(b, h, j):
                n = b * H * NSTEP + h * NSTEP + j
                sp.wait_ge(pv_done, SPARE + n - 3)
                sp.sem_inc(turn_go, 1)
                sp.wait_ge(hi_done, SPARE + n + 1)
                sp.sem_inc(turn_go, 1)
                sp.dma_start(pt_hi[:, j % 4], p_hi[:, j % 2, :], transpose=True).then_inc(hi_in[j % 2], 16)
                sp.wait_ge(lo_done, SPARE + n + 1)
                sp.sem_inc(turn_go, 1)
                sp.dma_start(pt_lo[:, j % 4], p_lo[:, j % 2, :], transpose=True).then_inc(lo_in[j % 2], 16)

            for b in range(B):
                if b == B - 1:
                    sp.wait_ge(kt_done, 8 * B)
                    sp.wait_ge(kn_done, KN_DONE)
                with sp.Fori(0, H) as h:
                    if b == B - 1:
                        sp.dma_start(wmix[:, bass.ts(h, D)], w_mix[:, bass.ts(h, D)]).then_inc(wmix_in, 16)
                    for j in range(NSTEP):
                        turn_exponents(b, h, j)

            sp.wait_ge(ctx_done, SPARE + NQT)
            sp.wait_ge(pv_done, SPARE + NCHUNK)
            sp.dma_start(wdn_raw[:, :, :].rearrange("p c n -> p (c n)"), w_dn).then_inc(wdn_in, 16)
            sp.dma_start(sgu[:, :, :].rearrange("p c n -> p (c n)"), s_gu).then_inc(wdn_in, 16)
            sp.dma_start(sdn[:, :], s_dn.partition_broadcast(P)).then_inc(wdn_in, 16)
            sp.wait_ge(acc_done, OUTS.index(("out", NT - 1)) + 1)
            n = 2 * DC * P
            for j in range(HC):
                sp.dma_start(wgu_raw[:, j * n:(j + 1) * n], w_gu[:, j * n:(j + 1) * n])\
                  .then_inc(wgu_in[j], 16)
            for t in range(NT):
                sp.wait_ge(y_ok, t + 1)
                sp.dma_start(out_v[:, t, :], xres[:, t, :]).then_inc(y_out, 16)
            sp.wait_ge(y_out, 16 * NT)

        @block.gpsimd
        def _(pool):
            nc.gpsimd.memset(ident[:, :], 0.0).then_inc(const_ok, 1)
            nc.gpsimd.memset(mhalf[:, :], -0.5).then_inc(const_ok, 1)
            pool.wait_ge(const_ok, 2)
            nc.gpsimd.affine_select(out=ident[:, :], in_=ident[:, :], compare_op=ALU.not_equal, fill=1.0,
                                    base=0, pattern=[[-1, P]], channel_multiplier=1).then_inc(const_ok, 1)
            for s in (q_ready, ctx_done):
                pool.sem_inc(s, SPARE)

            def inverse_root(t0, n, done):
                pool.wait_ge(var_ok, done)
                nc.gpsimd.tensor_tensor(rstd[:, t0:t0 + n], mv[:, t0:t0 + n, 1], mhalf[:, 0:n],
                                        ALU.pow).then_inc(rstd_ok, 1)

            def norm_root(norm):
                inverse_root(norm[1], 1, 2 + NORMS.index(norm))

            inverse_root(0, NT, 1)

            def kv_rope(p, i, k):
                pool.wait_ge(cs_in[i], 32 * k)
                kv = kvr[:, :, bass.ds(p * PIECE, PIECE)]
                halves = kv.rearrange("p b (k a d) -> p b k a d", a=2, d=P // 2)
                rot = krot[:, :, :].rearrange("p b (k a d) -> p b k a d", a=2, d=P // 2)
                sn = cs_k[:, i, 1, :].rearrange("p (k a d) -> p k a d", a=2, d=P // 2)
                for a in range(2):
                    nc.gpsimd.tensor_tensor(rot[:, :, :, a, :], halves[:, :, :, 1 - a, :],
                                            sn[:, :, a, :].unsqueeze(1).to_broadcast([P, B, PIECE // P, P // 2]),
                                            ALU.mult).then_inc(krope, 1)
                pool.drain()
                nc.gpsimd.tensor_tensor(kv, kv, cs_k[:, i, 0, :].unsqueeze(1).to_broadcast([P, B, PIECE]),
                                        ALU.mult).then_inc(krope, 1)
                pool.drain()
                nc.gpsimd.tensor_tensor(kv, kv, krot[:, :, :], ALU.add).then_inc(krope, 1)
                pool.drain()

            with pool.Fori(0, NP // 2) as pair:
                for q in range(4):
                    pool.wait_ge(kv_in[q], 16)
                kv_rope(2 * pair, 0, pair + 1)
                kv_rope(2 * pair + 1, 1, pair + 1)
            pool.wait_ge(kmax_ok, NP + 1)
            nc.gpsimd.partition_all_reduce(kmax[:, NP + 1:NP + 2], kmax[:, NP:NP + 1], P,
                                           bass.bass_isa.ReduceOp.max).then_inc(kmax_all, 1)

            def split_keys(b, p):
                cols = bass.ds(p * PIECE, PIECE)
                nc.gpsimd.tensor_tensor(kn_raw[:, :], kvr[:, b, cols], kscale.to_broadcast([P, PIECE]),
                                        ALU.mult).then_inc(knh_done, 1)
                pool.drain()
                nc.gpsimd.tensor_copy(kn_hi[b][:, cols], kn_raw[:, :]).then_inc(knh_done, 1)
                pool.drain()
                nc.gpsimd.tensor_tensor(kn_lo[b][:, cols], kn_raw[:, :], kn_hi[b][:, cols],
                                        ALU.subtract).then_inc(kn_done, 1)
                pool.drain()

            def split_query(t, i):
                pool.wait_ge(s_done, SPARE + NCH * t - NCH)
                q = qctx[:, bass.ds(t * P, P)]
                nc.gpsimd.tensor_copy(q_hi[:, i, :], q).then_inc(qh_done, 1)
                pool.drain()
                nc.gpsimd.tensor_tensor(q_lo[:, i, :], q, q_hi[:, i, :].bitcast(F32),
                                        ALU.subtract).then_inc(q_ready, 1)

            def sum_chunks(t, i):
                pool.wait_ge(o_used, SPARE + t + 1)
                nc.gpsimd.tensor_tensor(osum[:, :, :], oscl[:, i, 0:2, :], oscl[:, i, 2:4, :],
                                        ALU.add).then_inc(ctx_half, 1)
                pool.drain()
                nc.gpsimd.tensor_tensor(qctx[:, bass.ds(t * P, P)], osum[:, 0, :], osum[:, 1, :],
                                        ALU.add).then_inc(ctx_done, 1)
                pool.wait_ge(ctx_done, SPARE + t + 1)

            pool.wait_ge(kexp_ok, 4)
            with pool.Fori(0, NP) as p:
                split_keys(0, p)

            pool.wait_ge(d_done, H)
            split_query(0, 0)
            split_query(1, 1)
            pool.wait_ge(c_done, H)
            pool.wait_ge(qabs_ok, H)
            with pool.Fori(0, NP) as p:
                split_query(2 * p + 2, 0)
                sum_chunks(2 * p, 0)
                split_query(2 * p + 3, 1)
                sum_chunks(2 * p + 1, 1)
                split_keys(1, p)
            with pool.Fori(NP, NQT // 2 - 1) as pair:
                split_query(2 * pair + 2, 0)
                sum_chunks(2 * pair, 0)
                split_query(2 * pair + 3, 1)
                sum_chunks(2 * pair + 1, 1)
            norm_root(("x", 0))
            sum_chunks(NQT - 2, 0)
            sum_chunks(NQT - 1, 1)

            def mix_qk(t):
                for n, g in enumerate((1, 3)):
                    if n == 0:
                        pool.wait_ge(qkv_ok, t + 1)
                    q = qkv[:, t % 2, 0, :].rearrange("p (h d) -> p h d", d=DK)[:, g * HG:(g + 1) * HG, :]
                    k = qkv[:, t % 2, 1, :].rearrange("p (k d) -> p k d", d=DK)
                    if t:
                        pool.wait_ge(mix_dve, MIX_STEPS * (t - 1) + MIX_FREE[g])
                    nc.gpsimd.tensor_tensor(prod[:, 1 + n], q.unsqueeze(2).to_broadcast([P, HG, H, DK]),
                                            k.unsqueeze(1).to_broadcast([P, HG, H, DK]),
                                            ALU.mult).then_inc(mix_pool, 1)

            def mix_v(t):
                for n, g in enumerate((1, 3)):
                    v = qkv[:, t % 2, 2, :].rearrange("p (k d) -> p d k", d=DK)
                    pool.wait_ge(mix_dve, MIX_STEPS * t + MIX_SUM[g])
                    s = mix[:, g * HG:(g + 1) * HG, :]
                    o = prod[:, 1 + n].rearrange("p h k d -> p h (k d)").rearrange("p h (d k) -> p h d k", k=H)
                    nc.gpsimd.tensor_tensor(o, s.unsqueeze(2).to_broadcast([P, HG, DK, H]),
                                            v.unsqueeze(1).to_broadcast([P, HG, DK, H]),
                                            ALU.mult).then_inc(mix_pool, 1)

            for t in range(NT - 1):
                mix_qk(t)
                norm_root(("x", t + 1))
                mix_v(t)
                if t:
                    norm_root(("f", t - 1))
            mix_qk(3)
            norm_root(("f", 2))
            mix_v(3)
            norm_root(("f", 3))

        @block.scalar
        def _(act):
            act.wait_ge(x_in, 16)
            for q in range(4):
                cols = slice(q * L // 4, (q + 1) * L // 4)
                act.dma_start(kvr[:, :, cols], kv_v[:, :, cols]).then_inc(kv_in[q], 16)
            for s in (exp_done, hi_done, al_done):
                act.sem_inc(s, SPARE)
            for i in range(2):
                act.sem_inc(hi_in[i], 16 * SPARE)
            act.wait_ge(const_ok, 2)
            for c in range(DC):
                act.wait_ge(xnT_mm, c + 1)
                nc.scalar.copy(xnT_hi[:, c, :], ps_s[:, c, :]).then_inc(xnTh_ok, 1)

            def round_wq(i, k):
                act.wait_ge(wq_in[i], 16 * k)
                nc.scalar.copy(wq_hi[:, i, :, :], wq_s[:, i, :, :]).then_inc(wqh_ok, 1)

            def take_qhk(h, i):
                act.wait_ge(a_done, h + 1)
                nc.scalar.copy(qhk[:, i, :], ps_t[:, 0, :]).then_inc(qhk_ok, 1)

            def take_g_d(h, i):
                act.wait_ge(g_done, h + 1)
                nc.scalar.copy(gmat[:, i, :, :].rearrange("p c d -> p (c d)"), ps_t[:, 1, 0:DCQ]).then_inc(g_ok, 1)
                act.wait_ge(d_done, h + 1)
                nc.scalar.copy(wo_abs[:, bass.ds(h * D, D)], ps_o[:, 1, :]).then_inc(d_ok, 1)

            def take_qabs(h):
                act.wait_ge(c_done, h + 1)
                dst = qctx.rearrange("p (b c) -> p b c", b=B)[:, :, bass.ds(h * S, S)]
                nc.scalar.copy(dst, ps_o[:, 0, :].rearrange("p (b s) -> p b s", b=B)).then_inc(qabs_ok, 1)

            round_wq(0, 1)
            round_wq(1, 1)
            take_qhk(0, 0)
            take_qhk(1, 1)
            take_g_d(0, 0)
            with act.Fori(0, (H - 2) // 2) as pair:
                for h, i in ((2 * pair + 1, 1), (2 * pair + 2, 0)):
                    round_wq(1 - i, pair + 2)
                    take_qhk(h + 1, 1 - i)
                    take_g_d(h, i)
                    take_qabs(h - 1)
            take_g_d(H - 1, 1)
            take_qabs(H - 2)

            def key_columns(b, g):
                act.wait_ge(ktt_done, 8 * b + g + 1)
                nc.scalar.copy(kt_hi[:, g * HALF:(g + 1) * HALF], ps_t[:, g % 2, :]).then_inc(kth_done, 1)

            act.wait_ge(krope, 4 * NP)
            for g in range(4):
                key_columns(0, g)
            take_qabs(H - 1)
            for g in range(4, 8):
                key_columns(0, g)

            def take_hi(n, half, j):
                act.wait_ge(hi_in[j % 2], 16 * SPARE + 16 * half)
                act.wait_ge(exp_done, SPARE + n + 1)
                nc.scalar.mul(p_hi[:, j % 2, :], prob[:, j % 2, :], PSCALE).then_inc(hi_done, 1)

            def exponents(n, j):
                act.wait_ge(m_done, SPARE + n + 1)
                act.wait_ge(lo_done, SPARE + n - 1)
                i, c = (j // NCH) % 2, j % NCH
                nc.scalar.activation(prob[:, j % 2, :],
                                     ps_s[:, 2 * (j % 2):2 * (j % 2) + 2, :].rearrange("p a c -> p (a c)"),
                                     ACT.Exp, bias=nmax[:, i, c:c + 1], scale=1.0,
                                     accum_out=rsum[:, i, c:c + 1]).then_inc(exp_done, 1)

            def weights_of_chunks(t, i):
                act.wait_ge(nrow_done, SPARE + t + 1)
                nc.scalar.activation(alpha[:, i, :], nmax[:, i, :], ACT.Exp, bias=nrow[:, i, :],
                                     scale=-1.0).then_inc(al_done, 1)

            def take_t(n, dst):
                act.wait_ge(tr_done, n + 1)
                nc.scalar.copy(dst, ps_t[:, n % 2, :]).then_inc(tr_ok, 1)

            def ctx_columns(t):
                for g in range(4):
                    if g == 0 and t:
                        act.wait_ge(acc_done, OUTS.index(("out", t - 1)) + 1)
                    take_t(BANKS.index(("ctx", t, g)), ctxT[:, 4 * g:4 * g + 4, :].rearrange("p h s -> p (h s)"))

            def head(b, h, last):
                n0 = b * H * NSTEP + h * NSTEP
                for j in range(NSTEP):
                    if last and b == B - 1 and j == SIDE_STEP:
                        ctx_columns(0)
                    exponents(n0 + j, j)
                    take_hi(n0 + j, (b * H + h) * (NSTEP // 2) + j // 2, j)
                    if last and b < B - 1 and j in KEY_STEPS:
                        key_columns(b + 1, 2 * (j - KEY_STEPS[0]))
                        key_columns(b + 1, 2 * (j - KEY_STEPS[0]) + 1)
                    if j % NCH == NCH - 1:
                        weights_of_chunks(b * H * TPH + h * TPH + j // NCH, j // NCH)

            for b in range(B):
                with act.Fori(0, H - 1) as h:
                    head(b, h, False)
                if b == B - 1:
                    act.wait_ge(pv_done, SPARE + NCHUNK // B)
                    act.dma_start(xres[:, :, :], x_v).then_inc(x_again, 16)
                head(b, H - 1, True)

            def take_qkv(t):
                act.wait_ge(qkv_done, t + 1)
                if t >= 2:
                    act.wait_ge(mix_dve, MIX_STEPS * (t - 1))
                nc.scalar.copy(qkv[:, t % 2, :, :], ps_s[:, 0:3, :]).then_inc(qkv_ok, 1)

            def take_xT(t):
                if t >= 2:
                    act.wait_ge(qkv_done, t - 1)
                take_t(BANKS.index(("x", t)), ynT[:, t % 2, :, :].rearrange("p c s -> p (c s)"))

            def take_mixT(t):
                if t >= 2:
                    act.wait_ge(acc_done, OUTS.index(("mix", t - 2)) + 1)
                take_t(BANKS.index(("mix", t)),
                       mixT[:, 4 * (t % 2):4 * (t % 2) + 4, :].rearrange("p h s -> p (h s)"))

            def take_fT(t):
                if t >= 2:
                    act.wait_ge(f_done, HC)
                n = BANKS.index(("f", t))
                act.wait_ge(tr_done, n + 1)
                nc.scalar.copy(fnT_hi[:, :, t % 2, :],
                               ps_t[:, n % 2, :].rearrange("p (c s) -> p c s", c=DC)).then_inc(fh_ok, 1)

            def shift_gu(j):
                n = 2 * DC * P
                act.wait_ge(wgu_in[j], 16)
                cols = slice(j * n, (j + 1) * n)
                nc.scalar.activation(wgu[:, cols], wgu_raw[:, cols], ACT.Copy, bias=-ZERO_POINT, scale=1.0).then_inc(wgu_ok, 1)

            def shift_down():
                act.wait_ge(wdn_in, 16 * 3)
                w = wdn[:, :, :].rearrange("p c n -> p (c n)")
                raw = wdn_raw[:, :, :].rearrange("p c n -> p (c n)")
                n = HC * D // 4
                for k in range(4):
                    cols = slice(k * n, (k + 1) * n)
                    nc.scalar.activation(w[:, cols], raw[:, cols], ACT.Copy, bias=-ZERO_POINT, scale=1.0).then_inc(wdn_ok, 1)

            def silu_gate(p, j):
                n = HC * p + j
                act.wait_ge(f_done, n + 1)
                if n >= 2:
                    act.wait_ge(hid_ok, n - 1)
                nc.scalar.activation(gact[:, n % 2, :], ps_s[:, n % 4, 0:S], ACT.Silu,
                                     scale=sgu[:, j, 0:1]).then_inc(gact_ok, 1)

            def round_hidden(p, j):
                n = HC * p + j
                act.wait_ge(hid_ok, n + 1)
                if p:
                    act.wait_ge(acc_done, OUTS.index(("down", TPH - 1)) + 1)
                nc.scalar.copy(hT_hi[:, j * S:(j + 1) * S], hid[:, n % 2, :]).then_inc(hh_ok, 1)

            take_xT(0)
            take_qkv(0)
            ctx_columns(1)
            shift_down()
            take_xT(1)
            take_qkv(1)
            ctx_columns(2)
            take_mixT(0)
            take_xT(2)
            take_qkv(2)
            ctx_columns(3)
            take_mixT(1)
            take_xT(3)
            shift_gu(0)
            shift_gu(1)
            take_qkv(3)
            take_mixT(2)
            take_fT(0)
            take_fT(1)
            for j in range(HC):
                if j + 2 < HC:
                    shift_gu(j + 2)
                silu_gate(0, j)
                if j:
                    round_hidden(0, j - 1)
            round_hidden(0, HC - 1)
            take_fT(2)
            take_mixT(3)
            take_fT(3)
            for j in range(HC):
                silu_gate(1, j)
                if j:
                    round_hidden(1, j - 1)
            round_hidden(1, HC - 1)

        @block.vector
        def _(dve):
            dve.wait_ge(x_in, 16)
            for t in range(NT):
                nc.vector.bn_stats(stats[:, t, :], x_in1[:, t, :]).then_inc(st_ln, 1)
            for t in range(NT):
                dve.wait_ge(st_ln, t + 1)
                nc.vector.bn_aggr(mv[:, t, :], stats[:, t, :]).then_inc(st_ln, 1)
            dve.wait_ge(st_ln, 2 * NT)
            nc.vector.tensor_scalar(mv[:, :, 1], mv[:, :, 1], EPS, None, ALU.add).then_inc(var_ok, 1)
            dve.wait_ge(rstd_ok, 1)
            for t in range(NT):
                nc.vector.tensor_scalar(xn[:, t, :], x_in1[:, t, :], mv[:, t, 0:1], rstd[:, t:t + 1],
                                        ALU.subtract, ALU.mult).then_inc(xn_ok, 1)
            for s in (m_done, lo_done, nrow_done, o_used):
                dve.sem_inc(s, SPARE)
            for i in range(2):
                dve.sem_inc(lo_in[i], 16 * SPARE)

            def q_rope(h, i):
                dve.wait_ge(b_done, h + 1)
                q = ps_s[:, 0:QC, :].rearrange("p c (b s) -> p c b s", b=B)
                o = qcos[:, i, :, :].rearrange("p c (b s) -> p c b s", b=B)
                nc.vector.tensor_tensor(o, q, cosq[:, :, :].unsqueeze(2).to_broadcast([P, QC, B, S]), ALU.mult)
                r = qrot[:, i, :, :].rearrange("p c (b s) -> p c b s", b=B)
                for dst, src, p0, p1 in ((0, 1, slice(0, P), slice(0, P)), (1, 0, slice(0, P), slice(0, P)),
                                         (2, 2, slice(0, P // 2), slice(P // 2, P)),
                                         (2, 2, slice(P // 2, P), slice(0, P // 2))):
                    sn = sinq[p1, dst, :]
                    last = nc.vector.tensor_tensor(r[p0, dst, :, :], q[p1, src, :, :],
                                                   sn.unsqueeze(1).to_broadcast([sn.shape[0], B, S]), ALU.mult)
                last.then_inc(rope_mul, 1)
                dve.wait_ge(rope_mul, h + 1)
                nc.vector.tensor_tensor(qcos[:, i, :, :], qcos[:, i, :, :], qrot[:, i, :, :],
                                        ALU.add).then_inc(qrope_ok, 1)

            def largest_key(p):
                dve.wait_ge(krope, 4 * (p + 1))
                nc.vector.tensor_reduce(kmax[:, bass.ds(p, 1)], kvr[:, :, bass.ds(p * PIECE, PIECE)],
                                        mybir.AxisListType.XY, ALU.max,
                                        apply_absolute_value=True).then_inc(kmax_ok, 1)

            for c in range(DC):
                dve.wait_ge(xnTh_ok, c + 1)
                nc.vector.tensor_tensor(xnT_lo[:, c, :], ps_s[:, c, :], xnT_hi[:, c, :].bitcast(F32),
                                        ALU.subtract).then_inc(xnT_ok, 1)

            def wq_low(h, i):
                dve.wait_ge(wqh_ok, h + 1)
                nc.vector.tensor_tensor(wq_lo[:, i, :, :], wq_s[:, i, :, :], wq_hi[:, i, :, :].bitcast(F32),
                                        ALU.subtract).then_inc(wq_ok, 1)

            wq_low(0, 0)
            wq_low(1, 1)
            dve.wait_ge(tab_in, 32)
            q_rope(0, 0)
            with dve.Fori(0, NP // 2) as pair:
                wq_low(2 * pair + 2, 0)
                q_rope(2 * pair + 1, 1)
                largest_key(2 * pair)
                wq_low(2 * pair + 3, 1)
                q_rope(2 * pair + 2, 0)
                largest_key(2 * pair + 1)
            dve.wait_ge(kmax_ok, NP)
            nc.vector.tensor_reduce(kmax[:, NP:NP + 1], kmax[:, 0:NP], AX_X, ALU.max).then_inc(kmax_ok, 1)
            wq_low(NP + 2, 0)
            q_rope(NP + 1, 1)
            wq_low(NP + 3, 1)
            q_rope(NP + 2, 0)
            dve.wait_ge(kmax_all, 1)
            nc.vector.tensor_scalar(kexp[:, 0:1], kmax[:, NP + 1:NP + 2].bitcast(I32), EXP_BITS, None,
                                    ALU.bitwise_and).then_inc(kexp_ok, 1)
            dve.wait_ge(kexp_ok, 1)
            nc.vector.tensor_scalar(kexp[:, 1:2], kexp[:, 0:1], float(15 * EXP_ONE), -1.0, ALU.max,
                                    ALU.mult).then_inc(kexp_ok, 1)
            dve.wait_ge(kexp_ok, 2)
            nc.vector.tensor_scalar(kexp[:, 2:3], kexp[:, 1:2], float(268 * EXP_ONE), None,
                                    ALU.add).then_inc(kexp_ok, 1)
            nc.vector.tensor_scalar(kexp[:, 3:4], kexp[:, 1:2], -1.0, -float(14 * EXP_ONE), ALU.mult,
                                    ALU.add).then_inc(kexp_ok, 1)

            with dve.Fori(NP // 2 + 1, (H - 2) // 2) as pair:
                wq_low(2 * pair + 2, 0)
                q_rope(2 * pair + 1, 1)
                wq_low(2 * pair + 3, 1)
                q_rope(2 * pair + 2, 0)
            q_rope(H - 1, 1)

            def key_columns(b, g):
                dve.wait_ge(kth_done, 8 * b + g + 1)
                cols = slice(g * HALF, (g + 1) * HALF)
                nc.vector.tensor_tensor(kt_lo[:, cols], ps_t[:, g % 2, :], kt_hi[:, cols].bitcast(F32),
                                        ALU.subtract).then_inc(kt_done, 1)

            def take_lo(n, half, j):
                dve.wait_ge(lo_in[j % 2], 16 * SPARE + 16 * half)
                dve.wait_ge(hi_done, SPARE + n + 1)
                nc.vector.scalar_tensor_tensor(out=p_lo[:, j % 2, :], in0=prob[:, j % 2, :], scalar=PSCALE,
                                               in1=p_hi[:, j % 2, :], op0=ALU.mult,
                                               op1=ALU.subtract).then_inc(lo_done, 1)

            def chunk_maximum(n, j):
                dve.wait_ge(s_done, SPARE + n + 1)
                i, c = (j // NCH) % 2, j % NCH
                nc.vector.tensor_reduce(nmax[:, i, c:c + 1],
                                        ps_s[:, 2 * (j % 2):2 * (j % 2) + 2, :].rearrange("p a c -> p (a c)"),
                                        AX_X, ALU.max, negate=True).then_inc(m_done, 1)

            def row_maximum(t, i):
                dve.wait_ge(m_done, SPARE + NCH * (t + 1))
                nc.vector.tensor_reduce(nrow[:, i, :], nmax[:, i, :], AX_X, ALU.min).then_inc(nrow_done, 1)

            def row_sum(t, i):
                dve.wait_ge(al_done, SPARE + t + 1)
                nc.vector.tensor_tensor_reduce(out=junk[:, i, :], in0=alpha[:, i, :], in1=rsum[:, i, :], scale=PSCALE,
                                               scalar=0.0, op0=ALU.mult, op1=ALU.add,
                                               accum_out=lsum[:, i, :]).then_inc(fin, 1)

            def row_reciprocal(t, i):
                dve.wait_ge(fin, 3 * t + 1)
                nc.vector.reciprocal(lrec[:, i, :], lsum[:, i, :]).then_inc(fin, 1)

            def chunk_weights(t, i):
                dve.wait_ge(fin, 3 * t + 2)
                nc.vector.tensor_scalar(weigh[:, i, :], alpha[:, i, :], lrec[:, i, :], kunscale,
                                        ALU.mult, ALU.mult).then_inc(fin, 1)

            def weigh_chunks(t, i):
                dve.wait_ge(fin, 3 * t + 3)
                dve.wait_ge(pv_done, SPARE + NCH * (t + 1))
                dve.wait_ge(ctx_done, SPARE + t - 1)
                nc.vector.tensor_tensor(oscl[:, i, :, :], ps_o[:, i, :].rearrange("p (c d) -> p c d", c=NCH),
                                        weigh[:, i, :].unsqueeze(2).to_broadcast([P, NCH, P]),
                                        ALU.mult).then_inc(o_used, 1)

            def layer_norm(norm):
                k = NORMS.index(norm)
                kind, t = norm
                n = OUTS.index(("out", t) if kind == "x" else ("mix", t))
                dve.wait_ge(x_again, 16)
                dve.wait_ge(acc_done, n + 1)
                nc.vector.tensor_tensor(xres[:, t, :], ps_o[:, n % 2, :], xres[:, t, :], ALU.add).then_inc(acc_used, 1)
                dve.wait_ge(acc_used, n + 1)
                nc.vector.bn_stats(stats[:, t, :], xres[:, t, :]).then_inc(st_ln, 1)
                dve.wait_ge(st_ln, 2 * NT + 2 * k + 1)
                nc.vector.bn_aggr(mv[:, t, :], stats[:, t, :]).then_inc(st_ln, 1)
                dve.wait_ge(st_ln, 2 * NT + 2 * k + 2)
                nc.vector.tensor_scalar(mv[:, t, 1:2], mv[:, t, 1:2], EPS, None, ALU.add).then_inc(var_ok, 1)
                dve.wait_ge(rstd_ok, 2 + k)
                if k >= 2:
                    dve.wait_ge(tr_done, max(BANKS.index(NORMS[i]) for i in range(k) if NORMS[i][1] % 2 == t % 2) + 1)
                nc.vector.tensor_scalar(yn[:, t % 2, :], xres[:, t, :], mv[:, t, 0:1], rstd[:, t:t + 1],
                                        ALU.subtract, ALU.mult).then_inc(yn_ok, 1)

            def head(b, h, first, last):
                n0 = b * H * NSTEP + h * NSTEP
                t0 = b * H * TPH + h * TPH
                for j in range(NSTEP):
                    c, t, i = j % NCH, t0 - 1 + j // NCH, (j // NCH + 1) % 2
                    ends = not (first and j < NCH)
                    if c == 1 and ends:
                        row_sum(t, i)
                    if c == 2 and ends:
                        chunk_weights(t, i)
                    if c == 3 and ends:
                        weigh_chunks(t, i)
                    if last and b == B - 1 and j == SIDE_STEP:
                        layer_norm(("x", 0))
                    if not (last and b == B - 1 and j == NSTEP - 1):
                        chunk_maximum(n0 + j + 1, j + 1)
                    if c == 1 and ends:
                        row_reciprocal(t, i)
                    if c == NCH - 2:
                        row_maximum(t0 + j // NCH, j // NCH)
                    take_lo(n0 + j, (b * H + h) * (NSTEP // 2) + j // 2, j)
                    if last and b < B - 1 and j in KEY_STEPS:
                        key_columns(b + 1, 2 * (j - KEY_STEPS[0]))
                        key_columns(b + 1, 2 * (j - KEY_STEPS[0]) + 1)

            for g in range(8):
                key_columns(0, g)
            chunk_maximum(0, 0)
            for b in range(B):
                head(b, 0, b == 0, False)
                with dve.Fori(1, H - 1) as h:
                    head(b, h, False, False)
                head(b, H - 1, False, True)
            row_sum(NQT - 1, 1)
            row_reciprocal(NQT - 1, 1)
            chunk_weights(NQT - 1, 1)
            weigh_chunks(NQT - 1, 1)

            def mix_step(t, m):
                what, g = MIX_ORDER[m]
                heads = slice(g * HG, (g + 1) * HG)
                done = MIX_STEPS * t + m
                slot = 0 if g % 2 == 0 else 1 + g // 2
                by_k = prod[:, slot]
                by_d = by_k.rearrange("p h k d -> p h (k d)").rearrange("p h (d k) -> p h d k", k=H)
                if what == "mul":
                    if m == 0:
                        dve.wait_ge(qkv_ok, t + 1)
                    if done:
                        dve.wait_ge(mix_dve, done)
                    q = qkv[:, t % 2, 0, :].rearrange("p (h d) -> p h d", d=DK)[:, heads, :]
                    k = qkv[:, t % 2, 1, :].rearrange("p (k d) -> p k d", d=DK)
                    last = nc.vector.tensor_tensor(by_k, q.unsqueeze(2).to_broadcast([P, HG, H, DK]),
                                                   k.unsqueeze(1).to_broadcast([P, HG, H, DK]), ALU.mult)
                elif what == "sum":
                    if g % 2:
                        dve.wait_ge(mix_pool, 4 * t + 1 + g // 2)
                    dve.wait_ge(mix_dve, done)
                    last = nc.vector.tensor_reduce(mix[:, heads, :], by_k, AX_X, ALU.add)
                elif what == "mulv":
                    dve.wait_ge(mix_dve, done)
                    v = qkv[:, t % 2, 2, :].rearrange("p (k d) -> p d k", d=DK)
                    last = nc.vector.tensor_tensor(by_d, mix[:, heads, :].unsqueeze(2).to_broadcast([P, HG, DK, H]),
                                                   v.unsqueeze(1).to_broadcast([P, HG, DK, H]), ALU.mult)
                else:
                    if g % 2:
                        dve.wait_ge(mix_pool, 4 * t + 3 + g // 2)
                    dve.wait_ge(mix_dve, done)
                    if t >= 2:
                        dve.wait_ge(tr_done, BANKS.index(("mix", t - 2)) + 1)
                    o = mixo[:, t % 2, :].rearrange("p (h d) -> p h d", d=DK)[:, heads, :]
                    last = nc.vector.tensor_reduce(o, by_d, AX_X, ALU.add)
                last.then_inc(mix_dve, 1)

            def norm_low(t):
                n = BANKS.index(("f", t))
                dve.wait_ge(fh_ok, t + 1)
                nc.vector.tensor_tensor(fnT_lo[:, :, t % 2, :], ps_t[:, n % 2, :].rearrange("p (c s) -> p c s", c=DC),
                                        fnT_hi[:, :, t % 2, :].bitcast(F32), ALU.subtract).then_inc(tr_ok, 1)

            def gate_up(p, j):
                n = HC * p + j
                dve.wait_ge(gact_ok, n + 1)
                if n >= 2:
                    dve.wait_ge(h_ok, n - 1)
                nc.vector.scalar_tensor_tensor(out=hid[:, n % 2, :], in0=ps_s[:, n % 4, S:2 * S],
                                               scalar=sgu[:, j, 1:2], in1=gact[:, n % 2, :], op0=ALU.mult,
                                               op1=ALU.mult).then_inc(hid_ok, 1)

            def hidden_low(p, j):
                n = HC * p + j
                dve.wait_ge(hh_ok, n + 1)
                cols = slice(j * S, (j + 1) * S)
                nc.vector.tensor_tensor(hT_lo[:, cols], hid[:, n % 2, :], hT_hi[:, cols].bitcast(F32),
                                        ALU.subtract).then_inc(h_ok, 1)

            def finish(t):
                n = OUTS.index(("down", t))
                dve.wait_ge(acc_done, n + 1)
                if t:
                    dve.wait_ge(y_ok, t)
                nc.vector.tensor_tensor(dsc[:, :], ps_o[:, n % 2, :], sdn[:, :], ALU.mult).then_inc(acc_used, 1)
                dve.wait_ge(acc_used, n + 1)
                nc.vector.tensor_tensor(xres[:, t, :], dsc[:, :], xres[:, t, :], ALU.add).then_inc(y_ok, 1)

            h_next = 0
            dve.wait_ge(ctx_done, SPARE + NQT)
            for t in range(NT - 1):
                for m in range(MIX_STEPS):
                    mix_step(t, m)
                    if m == MIX_STEPS // 2 - 1:
                        layer_norm(("x", t + 1))
                if t:
                    layer_norm(("f", t - 1))
            dve.wait_ge(wdn_in, 16 * 3)
            for m in range(MIX_STEPS):
                mix_step(3, m)
                if m < 2:
                    norm_low(m)
                elif m == 3:
                    layer_norm(("f", 2))
                elif h_next < HC:
                    gate_up(0, h_next)
                    if h_next:
                        hidden_low(0, h_next - 1)
                    h_next += 1
            for j in range(h_next, HC):
                gate_up(0, j)
                hidden_low(0, j - 1)
            hidden_low(0, HC - 1)
            norm_low(2)
            layer_norm(("f", 3))
            finish(0)
            finish(1)
            norm_low(3)
            for j in range(HC):
                gate_up(1, j)
                if j:
                    hidden_low(1, j - 1)
            hidden_low(1, HC - 1)
            finish(2)
            finish(3)

        @block.tensor
        def _(pe):
            for s in (s_done, pv_done):
                pe.sem_inc(s, SPARE)
            pe.wait_ge(const_ok, 3)
            pe.wait_ge(xn_ok, NT)
            for c in range(DC):
                for t in range(NT):
                    last = nc.tensor.transpose(ps_s[:, c, t * P:(t + 1) * P], xn[:, t, c * P:(c + 1) * P], ident[:, :])
                last.then_inc(xnT_mm, 1)
            pe.wait_ge(xnT_ok, DC)

            def q_head(h, i, first=False):
                pe.wait_ge(wq_ok, h + 1)
                if not first:
                    pe.wait_ge(qhk_ok, h)
                for c in range(DC):
                    nc.tensor.matmul(ps_t[:, 0, :], wq_hi[:, i, c, :], xnT_hi[:, c, :], start=(c == 0), stop=False)
                    nc.tensor.matmul(ps_t[:, 0, :], wq_hi[:, i, c, :], xnT_lo[:, c, :], start=False, stop=False)
                    last = nc.tensor.matmul(ps_t[:, 0, :], wq_lo[:, i, c, :], xnT_hi[:, c, :], start=False,
                                            stop=(c == DC - 1))
                last.then_inc(a_done, 1)

            def q_wide(h, i, k, first=False):
                pe.wait_ge(wkcq_in[i], 16 * k)
                pe.wait_ge(qhk_ok, h + 1)
                if not first:
                    pe.wait_ge(rope_mul, h)
                for c in range(QC):
                    last = nc.tensor.matmul(ps_s[:, c, :], wkcq_s[:, i, c * P:(c + 1) * P], qhk[:, i, :],
                                            start=True, stop=True)
                last.then_inc(b_done, 1)

            def fused_weights(h, i, k, first=False):
                pe.wait_ge(wrest_in[i], 64 * k)
                if not first:
                    pe.wait_ge(g_ok, h)
                for c in range(QC):
                    last = nc.tensor.matmul(ps_t[:, 1, c * P:(c + 1) * P], wqr_s[:, i, c * P:(c + 1) * P],
                                            wkr_s[:, i, :], start=True, stop=True)
                last.then_inc(g_done, 1)
                if not first:
                    pe.wait_ge(d_ok, h)
                nc.tensor.matmul(ps_o[:, 1, :], wkckv_s[:, i, :], wot_s[:, i, :],
                                 start=True, stop=True).then_inc(d_done, 1)

            def q_absorbed(h, i, first=False):
                pe.wait_ge(qrope_ok, h + 1)
                pe.wait_ge(g_ok, h + 1)
                if not first:
                    pe.wait_ge(qabs_ok, h)
                for c in range(QC):
                    last = nc.tensor.matmul(ps_o[:, 0, :], gmat[:, i, c, :], qcos[:, i, c, :],
                                            start=(c == 0), stop=(c == QC - 1))
                last.then_inc(c_done, 1)

            q_head(0, 0, True)
            q_wide(0, 0, 1, True)
            q_head(1, 1)
            fused_weights(0, 0, 1, True)
            q_wide(1, 1, 1)
            q_head(2, 0)
            fused_weights(1, 1, 1)
            q_absorbed(0, 0, True)
            with pe.Fori(0, (H - 4) // 2) as pair:
                for h, i, k in ((2 * pair + 2, 0, pair + 2), (2 * pair + 3, 1, pair + 2)):
                    q_wide(h, i, k)
                    q_head(h + 1, 1 - i)
                    fused_weights(h, i, k)
                    q_absorbed(h - 1, 1 - i)
            q_wide(H - 2, 0, H // 2)
            q_head(H - 1, 1)
            fused_weights(H - 2, 0, H // 2)
            q_absorbed(H - 3, 1)
            q_wide(H - 1, 1, H // 2)
            fused_weights(H - 1, 1, H // 2)
            q_absorbed(H - 2, 0)

            def key_columns(b, g):
                for k in range(4):
                    blk = 4 * g + k
                    last = nc.tensor.transpose(ps_t[:, g % 2, k * P:(k + 1) * P],
                                               kvr[:, b, blk * P:(blk + 1) * P], ident[:, :])
                last.then_inc(ktt_done, 1)

            pe.wait_ge(krope, 4 * NP)
            pe.wait_ge(qhk_ok, H)
            pe.wait_ge(g_ok, H)
            for g in range(4):
                if g >= 2:
                    pe.wait_ge(kt_done, g - 1)
                key_columns(0, g)
            q_absorbed(H - 1, 1)
            for g in range(4, 8):
                pe.wait_ge(kt_done, g - 1)
                key_columns(0, g)

            def scores(n, j):
                pe.wait_ge(exp_done, SPARE + n - 1)
                i, c = (j // NCH) % 2, j % NCH
                for a in range(2):
                    o = ps_s[:, 2 * (j % 2) + a, :]
                    cols = slice(c * CHUNK + a * HALF, c * CHUNK + (a + 1) * HALF)
                    nc.tensor.matmul(o, q_hi[:, i, :], kt_hi[:, cols], start=True, stop=False)
                    nc.tensor.matmul(o, q_hi[:, i, :], kt_lo[:, cols], start=False, stop=False)
                    last = nc.tensor.matmul(o, q_lo[:, i, :], kt_hi[:, cols], start=False, stop=True)
                last.then_inc(s_done, 1)

            def weighed_keys(b, half, t, j):
                i, c = (j // NCH) % 2, j % NCH
                if c == 0:
                    pe.wait_ge(o_used, SPARE + t - 1)
                o = ps_o[:, i, c * P:(c + 1) * P]
                pe.wait_ge(hi_in[j % 2], 16 * SPARE + 16 * (half + 1))
                for k in range(CHUNK // P):
                    keys = slice((c * (CHUNK // P) + k) * P, (c * (CHUNK // P) + k + 1) * P)
                    nc.tensor.matmul(o, pt_hi[:, j % 4, k, :], kn_hi[b][:, keys], start=(k == 0), stop=False)
                    nc.tensor.matmul(o, pt_hi[:, j % 4, k, :], kn_lo[b][:, keys], start=False, stop=False)
                pe.wait_ge(lo_in[j % 2], 16 * SPARE + 16 * (half + 1))
                for k in range(CHUNK // P):
                    keys = slice((c * (CHUNK // P) + k) * P, (c * (CHUNK // P) + k + 1) * P)
                    last = nc.tensor.matmul(o, pt_lo[:, j % 4, k, :], kn_hi[b][:, keys], start=False,
                                            stop=(k == CHUNK // P - 1))
                last.then_inc(pv_done, 1)

            def turn(bank, src, ready, count):
                n = BANKS.index(bank)
                pe.wait_ge(ready, count)
                if n >= 2:
                    pe.wait_ge(tr_ok, n - 1)
                for k in range(4):
                    last = nc.tensor.transpose(ps_t[:, n % 2, k * P:(k + 1) * P], src(k), ident[:, :])
                last.then_inc(tr_done, 1)

            def ready_out(n):
                if n == 0:
                    pe.wait_ge(o_used, SPARE + NQT - 3)
                elif n == 1:
                    pe.wait_ge(o_used, SPARE + NQT)
                else:
                    pe.wait_ge(acc_used, n - 1)
                return ps_o[:, n % 2, :]

            def context_out(t):
                for g in range(4):
                    turn(("ctx", t, g), lambda k: qctx[:, ctx_tile(t, 4 * g + k):ctx_tile(t, 4 * g + k) + P],
                         ctx_done, SPARE + NQT // B * (t // TPH + 1))
                pe.wait_ge(tr_ok, BANKS.index(("ctx", t, 3)) + 1)
                o = ready_out(OUTS.index(("out", t)))
                for h in range(H):
                    last = nc.tensor.matmul(o, ctxT[:, h, :], wo_abs[:, h * D:(h + 1) * D],
                                            start=(h == 0), stop=(h == H - 1))
                last.then_inc(acc_done, 1)

            def head(b, h, first, last):
                n0 = b * H * NSTEP + h * NSTEP
                t0 = b * H * TPH + h * TPH
                for j in range(NSTEP):
                    if not (last and b == B - 1 and j >= NSTEP - AHEAD):
                        if (j + AHEAD) % NCH == 0:
                            pe.wait_ge(q_ready, SPARE + t0 + (j + AHEAD) // NCH + 1)
                        if last and j >= NSTEP - AHEAD:
                            pe.wait_ge(kt_done, 8 * (b + 1) + 2 * (j - NSTEP + AHEAD + 1))
                        scores(n0 + j + AHEAD, j + AHEAD)
                    if last and b < B - 1 and j < NCH:
                        for g in (2 * j, 2 * j + 1):
                            pe.wait_ge(kt_done, 8 * (b + 1) + g - 1)
                            key_columns(b + 1, g)
                    if first and j < NCH:
                        pe.wait_ge(kn_done, 2 * (j + 1) if b == 0 else KN_DONE)
                    weighed_keys(b, (b * H + h) * (NSTEP // 2) + j // 2, t0 + j // NCH, j)

            pe.wait_ge(rope_mul, H)
            pe.wait_ge(q_ready, SPARE + 1)
            for n in range(AHEAD):
                pe.wait_ge(kt_done, 2 * (n + 1))
                scores(n, n)
            pe.wait_ge(qabs_ok, H)
            pe.wait_ge(d_ok, H)
            for b in range(B):
                head(b, 0, True, False)
                with pe.Fori(1, H - 1) as h:
                    head(b, h, False, False)
                if b == B - 1:
                    context_out(0)
                    pe.wait_ge(acc_used, 1)
                head(b, H - 1, False, True)

            def turn_norm(kind, t):
                turn((kind, t), lambda c: yn[:, t % 2, c * P:(c + 1) * P], yn_ok,
                     NORMS.index((kind, t)) + 1)

            def mix_in(t):
                pe.wait_ge(tr_ok, BANKS.index(("x", t)) + 1)
                pe.wait_ge(wmix_in, 16 * H)
                if t:
                    pe.wait_ge(qkv_ok, t)
                for m in range(3):
                    for c in range(DC):
                        last = nc.tensor.matmul(ps_s[:, m, :], ynT[:, t % 2, c, :],
                                                wmix[:, (m * DC + c) * D:(m * DC + c + 1) * D],
                                                start=(c == 0), stop=(c == DC - 1))
                last.then_inc(qkv_done, 1)

            def mix_out(t):
                turn(("mix", t), lambda c: mixo[:, t % 2, c * P:(c + 1) * P], mix_dve, MIX_STEPS * (t + 1))
                pe.wait_ge(tr_ok, BANKS.index(("mix", t)) + 1)
                o = ready_out(OUTS.index(("mix", t)))
                for c in range(DC):
                    last = nc.tensor.matmul(o, mixT[:, 4 * (t % 2) + c, :],
                                            wmix[:, (3 * DC + c) * D:(3 * DC + c + 1) * D],
                                            start=(c == 0), stop=(c == DC - 1))
                last.then_inc(acc_done, 1)

            def gate_up(p):
                pe.wait_ge(tr_ok, BANKS.index(("f", 2 * p + 1)) + 1)
                for j in range(HC):
                    n = HC * p + j
                    pe.wait_ge(wgu_ok, j + 1)
                    if n >= 4:
                        pe.wait_ge(hid_ok, n - 3)
                    else:
                        pe.wait_ge(qkv_ok, NT)
                    for m in range(2):
                        for c in range(DC):
                            w = wgu[:, ((2 * j + m) * DC + c) * P:((2 * j + m) * DC + c + 1) * P]
                            o = ps_s[:, n % 4, m * S:(m + 1) * S]
                            nc.tensor.matmul(o, w, fnT_hi[:, c, :, :].rearrange("p u s -> p (u s)"),
                                             start=(c == 0), stop=False)
                            last = nc.tensor.matmul(o, w, fnT_lo[:, c, :, :].rearrange("p u s -> p (u s)"),
                                                    start=False, stop=(c == DC - 1))
                    last.then_inc(f_done, 1)

            def down(t):
                pe.wait_ge(h_ok, HC * (t // TPH + 1))
                pe.wait_ge(wdn_ok, 4)
                o = ready_out(OUTS.index(("down", t)))
                for j in range(HC):
                    rows = slice(j * S + (t % TPH) * P, j * S + (t % TPH + 1) * P)
                    nc.tensor.matmul(o, hT_hi[:, rows], wdn[:, j, :], start=(j == 0), stop=False)
                    last = nc.tensor.matmul(o, hT_lo[:, rows], wdn[:, j, :], start=False,
                                            stop=(j == HC - 1))
                last.then_inc(acc_done, 1)

            turn_norm("x", 0)
            mix_in(0)
            for t in range(1, NT):
                context_out(t)
                if t >= 2:
                    mix_out(t - 2)
                turn_norm("x", t)
                mix_in(t)
            mix_out(2)
            turn_norm("f", 0)
            turn_norm("f", 1)
            gate_up(0)
            turn_norm("f", 2)
            mix_out(3)
            down(0)
            down(1)
            turn_norm("f", 3)
            gate_up(1)
            down(2)
            down(3)


MIX_ORDER = [("mul", 0), ("sum", 0), ("mul", 2), ("sum", 2), ("sum", 1), ("sum", 3),
             ("mulv", 0), ("sumv", 0), ("mulv", 2), ("sumv", 2), ("sumv", 1), ("sumv", 3)]
MIX_STEPS = len(MIX_ORDER)
MIX_SUM = {g: MIX_ORDER.index(("sum", g)) + 1 for g in range(4)}
MIX_FREE = {g: MIX_ORDER.index(("sumv", g)) + 1 for g in range(4)}
KEY_STEPS = range(3, 7)

SIDE_STEP = 3

BANKS = [("ctx", 0, g) for g in range(4)] + [("x", 0)]
for _t in range(1, NT):
    BANKS += [("ctx", _t, g) for g in range(4)] + ([("mix", _t - 2)] if _t >= 2 else []) + [("x", _t)]
BANKS += [("mix", 2), ("f", 0), ("f", 1), ("f", 2), ("mix", 3), ("f", 3)]
OUTS = [("out", 0), ("out", 1), ("out", 2), ("mix", 0), ("out", 3), ("mix", 1), ("mix", 2), ("mix", 3),
        ("down", 0), ("down", 1), ("down", 2), ("down", 3)]
NORMS = [("x", 0), ("x", 1), ("x", 2), ("f", 0), ("x", 3), ("f", 1), ("f", 2), ("f", 3)]


def ctx_tile(t, h):
    return ((t // TPH * H + h) * TPH + t % TPH) * P


def rope_tables(length, dim):
    inv = (np.float32(1.0) / np.power(np.float32(10000.0), np.arange(0, dim, 2, dtype=np.float32)
                                      / np.float32(dim)).astype(np.float32)).astype(np.float32)
    f = (np.arange(length, dtype=np.float32)[:, None] * inv[None, :]).astype(np.float32)
    sin = np.repeat(np.sin(f), 2, axis=-1).astype(np.float32)
    cos = np.repeat(np.cos(f), 2, axis=-1).astype(np.float32)
    sin[:, :dim // 2] *= -1
    return sin, cos


def kernel(x, ctx_512, L0_xattn_Wq, L0_xattn_w_kc_q, L0_xattn_w_kc_kv, L0_xattn_W_qr, L0_xattn_W_kr,
           L0_xattn_Wo, L0_attn_Wq, L0_attn_Wk, L0_attn_Wv, L0_attn_Wo, L0_ffn_wq_gate, L0_ffn_s_gate,
           L0_ffn_wq_up, L0_ffn_s_up, L0_ffn_wq_down, L0_ffn_s_down):
    import concourse.bacc as bacc
    from concourse.bass_utils import run_bass_kernel_spmd

    half = DCQ // 2
    perm = np.concatenate([np.arange(0, P), np.arange(half, half + P), np.arange(P, half),
                           np.arange(half + P, DCQ)])
    sin, cos = rope_tables(S, DCQ)
    cos_q = cos.T[perm].reshape(QC, P, S).transpose(1, 0, 2).reshape(P, QC * S)
    sq = sin.T[perm].reshape(QC, P, S)
    sq = np.stack([sq[0], sq[1], np.concatenate([sq[2, P // 2:], sq[2, :P // 2]])])
    sin_q = sq.transpose(1, 0, 2).reshape(P, QC * S)
    sin, cos = rope_tables(L, P)
    gate = np.asarray(L0_ffn_wq_gate).T.reshape(DC, P, HC, P)
    up = np.asarray(L0_ffn_wq_up).T.reshape(DC, P, HC, P)
    ins = {
        "x": x,
        "ctx_kv": ctx_512,
        "wq_t": np.asarray(L0_xattn_Wq).reshape(H, P, DC, P).transpose(0, 3, 2, 1).reshape(H, P, DC * P),
        "w_kcq": np.asarray(L0_xattn_w_kc_q)[:, :, perm],
        "w_qr_t": np.asarray(L0_xattn_W_qr)[:, perm, :].transpose(0, 2, 1),
        "w_kr_t": np.asarray(L0_xattn_W_kr).transpose(0, 2, 1),
        "w_kckv": L0_xattn_w_kc_kv,
        "wo_t": np.asarray(L0_xattn_Wo).T.reshape(H, P, D),
        "cos_q": cos_q,
        "sin_q": sin_q,
        "cos_k": cos.reshape(P, L),
        "sin_k": sin.reshape(P, L),
        "w_mix": np.concatenate([np.asarray(w).reshape(DC, P, D).transpose(1, 0, 2).reshape(P, DC * D)
                                 for w in (L0_attn_Wq, L0_attn_Wk, L0_attn_Wv, L0_attn_Wo)], axis=1),
        "w_gu": np.stack([gate, up]).transpose(2, 3, 0, 1, 4).reshape(P, HC * 2 * DC * P),
        "w_dn": np.asarray(L0_ffn_wq_down).T.reshape(HC, P, D).transpose(1, 0, 2).reshape(P, HC * D),
        "s_gu": np.stack([np.asarray(L0_ffn_s_gate), np.asarray(L0_ffn_s_up)], axis=-1)
                  .reshape(HC, P, 2).transpose(1, 0, 2).reshape(P, HC * 2),
        "s_dn": L0_ffn_s_down,
    }
    nc = bacc.Bacc("TRN2", target_bir_lowering=False, num_devices=1)
    arrays, aps = {}, {}
    for name, a in ins.items():
        a = np.ascontiguousarray(a)
        arrays[f"{name}_dram"] = a
        aps[name] = nc.dram_tensor(f"{name}_dram", list(a.shape), mybir.dt.from_np(a.dtype), kind="ExternalInput").ap()
    out = nc.dram_tensor("out_dram", [B, S, D], F32, kind="ExternalOutput").ap()
    build(nc, out=out, **aps)
    r = run_bass_kernel_spmd(nc, [arrays], core_ids=[0])
    return r.results[0]["out_dram"]
```
